# Optimizing a Trainium2 kernel written in Bass

```python
import numpy as np
import jax
import jax.numpy as jnp

def _softmax(x, axis=-1):
    return jax.nn.softmax(x, axis=axis)

def _gelu(x):
    return jax.nn.gelu(x, approximate=True)

def _silu(x):
    return jax.nn.silu(x)

def _sigmoid(x):
    return jax.nn.sigmoid(x)

def _layernorm(x, axis=-1, eps=1e-05):
    m = jnp.mean(x, axis=axis, keepdims=True)
    v = jnp.var(x, axis=axis, keepdims=True)
    return (x - m) / jnp.sqrt(v + eps)

def _scatter_add(tgt, idx, src, axis=0):
    return tgt.at[idx].add(src)

def _segment_sum(src, seg, n):
    return jax.ops.segment_sum(src, seg, n)
kernel_name = 'mk_gnn_preln_d2_gnn_r64_a1a65b'

def setup_inputs(seed: int=0):
    np.random.seed(seed)
    _w = jnp.asarray

    def _rec_inputs():
        import jax
        import jax.numpy as jnp
        _gk = jax.random.key(seed)
        x = -0.0001006 + 1 * jax.random.normal(jax.random.fold_in(_gk, 1), (50000, 96), jnp.float32)
        src = jax.random.randint(jax.random.fold_in(_gk, 2), (12500,), 0, 50000, jnp.int32)
        dst = jnp.minimum((50000 * jax.random.uniform(jax.random.fold_in(_gk, 3), (12500,)) ** 2.0).astype(jnp.int32), 49999)
        _o = jnp.argsort(dst, stable=True)
        src = src[_o]
        dst = dst[_o]
        edge_attr_96 = 5.93493e-05 + 1.00006 * jax.random.normal(jax.random.fold_in(_gk, 11), (12500, 96), jnp.float32)
        return (x, src, dst, edge_attr_96)
    x, src, dst, edge_attr_96 = _rec_inputs()

    def _L0_gnn_setup():
        import jax, jax.numpy as jnp
        import numpy as np
        N_NODES = 50000
        N_EDGES = 12500
        C = 96
        L = 3

        def _gru_cell(m, h, w_ih, w_hh, b_ih, b_hh):
            gi = m @ w_ih.T + b_ih
            gh = h @ w_hh.T + b_hh
            i_r, i_z, i_n = jnp.split(gi, 3, axis=-1)
            h_r, h_z, h_n = jnp.split(gh, 3, axis=-1)
            r = jax.nn.sigmoid(i_r + h_r)
            z = jax.nn.sigmoid(i_z + h_z)
            n = jnp.tanh(i_n + r * h_n)
            return (1.0 - z) * n + z * h
        key = jax.random.key(seed)
        ks = jax.random.split(key, 7)
        x = jax.random.normal(ks[0], (N_NODES, C), dtype=jnp.float32)
        edge_index = jax.random.randint(ks[1], (2, N_EDGES), 0, N_NODES, dtype=jnp.int32)
        weight = jax.random.normal(ks[2], (L, C, C), dtype=jnp.float32) * (1.0 / np.sqrt(C))
        w_ih = jax.random.normal(ks[3], (3 * C, C), dtype=jnp.float32) * (1.0 / np.sqrt(C))
        w_hh = jax.random.normal(ks[4], (3 * C, C), dtype=jnp.float32) * (1.0 / np.sqrt(C))
        b_ih = jax.random.normal(ks[5], (3 * C,), dtype=jnp.float32) * 0.01
        b_hh = jax.random.normal(ks[6], (3 * C,), dtype=jnp.float32) * 0.01
        return {'x': x, 'edge_index': edge_index, 'weight': weight, 'w_ih': w_ih, 'w_hh': w_hh, 'b_ih': b_ih, 'b_hh': b_hh}
    _L0_gnn_all = _L0_gnn_setup()
    _L0_gnn_in = {k: v for k, v in _L0_gnn_all.items() if k in ('weight', 'w_ih', 'w_hh', 'b_ih', 'b_hh')}
    del _L0_gnn_all

    def _L1_gnn_setup():
        import jax, jax.numpy as jnp
        import numpy as np
        N_NODES = 50000
        N_EDGES = 12500
        IN_DIM = 96
        NUM_HEADS = 8
        HEAD_DIM = IN_DIM // NUM_HEADS
        key = jax.random.key(seed)
        ks = jax.random.split(key, 11)
        s = 1.0 / np.sqrt(IN_DIM)
        return {'x': jax.random.normal(ks[0], (N_NODES, IN_DIM), dtype=jnp.float32), 'edge_index': jax.random.randint(ks[1], (2, N_EDGES), 0, N_NODES, dtype=jnp.int64), 'edge_attr': jax.random.normal(ks[2], (N_EDGES, IN_DIM), dtype=jnp.float32), 'Wq': jax.random.normal(ks[3], (IN_DIM, IN_DIM), dtype=jnp.float32) * s, 'bq': jax.random.normal(ks[4], (IN_DIM,), dtype=jnp.float32) * s, 'Wk': jax.random.normal(ks[5], (IN_DIM, IN_DIM), dtype=jnp.float32) * s, 'bk': jax.random.normal(ks[6], (IN_DIM,), dtype=jnp.float32) * s, 'We': jax.random.normal(ks[7], (IN_DIM, IN_DIM), dtype=jnp.float32) * s, 'be': jax.random.normal(ks[8], (IN_DIM,), dtype=jnp.float32) * s, 'Wv': jax.random.normal(ks[9], (IN_DIM, IN_DIM), dtype=jnp.float32) * s, 'bv': jax.random.normal(ks[10], (IN_DIM,), dtype=jnp.float32) * s}
    _L1_gnn_all = _L1_gnn_setup()
    _L1_gnn_in = {k: v for k, v in _L1_gnn_all.items() if k in ('Wq', 'bq', 'Wk', 'bk', 'We', 'be', 'Wv', 'bv')}
    del _L1_gnn_all
    return {'x': x, 'src': src, 'dst': dst, 'edge_attr_96': edge_attr_96, 'L0_gnn_weight': _L0_gnn_in['weight'], 'L0_gnn_w_ih': _L0_gnn_in['w_ih'], 'L0_gnn_w_hh': _L0_gnn_in['w_hh'], 'L0_gnn_b_ih': _L0_gnn_in['b_ih'], 'L0_gnn_b_hh': _L0_gnn_in['b_hh'], 'L1_gnn_Wq': _L1_gnn_in['Wq'], 'L1_gnn_bq': _L1_gnn_in['bq'], 'L1_gnn_Wk': _L1_gnn_in['Wk'], 'L1_gnn_bk': _L1_gnn_in['bk'], 'L1_gnn_We': _L1_gnn_in['We'], 'L1_gnn_be': _L1_gnn_in['be'], 'L1_gnn_Wv': _L1_gnn_in['Wv'], 'L1_gnn_bv': _L1_gnn_in['bv']}

def reference(x, src, dst, edge_attr_96, L0_gnn_weight, L0_gnn_w_ih, L0_gnn_w_hh, L0_gnn_b_ih, L0_gnn_b_hh, L1_gnn_Wq, L1_gnn_bq, L1_gnn_Wk, L1_gnn_bk, L1_gnn_We, L1_gnn_be, L1_gnn_Wv, L1_gnn_bv):
    import jax
    import jax.numpy as jnp

    def _L0_gnn_ref(x, edge_index, weight, w_ih, w_hh, b_ih, b_hh):
        import jax, jax.numpy as jnp
        import numpy as np
        N_NODES = 50000
        N_EDGES = 12500
        C = 96
        L = 3

        def _gru_cell(m, h, w_ih, w_hh, b_ih, b_hh):
            gi = m @ w_ih.T + b_ih
            gh = h @ w_hh.T + b_hh
            i_r, i_z, i_n = jnp.split(gi, 3, axis=-1)
            h_r, h_z, h_n = jnp.split(gh, 3, axis=-1)
            r = jax.nn.sigmoid(i_r + h_r)
            z = jax.nn.sigmoid(i_z + h_z)
            n = jnp.tanh(i_n + r * h_n)
            return (1.0 - z) * n + z * h
        src = edge_index[0]
        dst = edge_index[1]
        for i in range(L):
            m = x @ weight[i]
            agg = jax.ops.segment_sum(m[src], dst, num_segments=N_NODES)
            x = _gru_cell(agg, x, w_ih, w_hh, b_ih, b_hh)
        return x

    def _L1_gnn_ref(x, edge_index, edge_attr, Wq, bq, Wk, bk, We, be, Wv, bv):
        import jax, jax.numpy as jnp
        import numpy as np
        N_NODES = 50000
        N_EDGES = 12500
        IN_DIM = 96
        NUM_HEADS = 8
        HEAD_DIM = IN_DIM // NUM_HEADS
        N = x.shape[0]
        H, D = (NUM_HEADS, HEAD_DIM)
        Q_h = (x @ Wq + bq).reshape(N, H, D)
        K_h = (x @ Wk + bk).reshape(N, H, D)
        V_h = (x @ Wv + bv).reshape(N, H, D)
        E = (edge_attr @ We + be).reshape(-1, H, D)
        src_idx = edge_index[0]
        dst_idx = edge_index[1]
        src = K_h[src_idx]
        dest = Q_h[dst_idx]
        score = src * dest / jnp.sqrt(jnp.asarray(D, x.dtype))
        score = score * E
        score = jnp.exp(jnp.clip(score.sum(-1, keepdims=True), -5.0, 5.0))
        msg = V_h[src_idx] * score
        wV = jax.ops.segment_sum(msg, dst_idx, num_segments=N)
        Z = jax.ops.segment_sum(score, dst_idx, num_segments=N)
        h_out = wV / (Z + 1e-06)
        return h_out.reshape(N, H * D)
    edge_index = jnp.stack([src, dst])
    h = jnp.maximum(_layernorm(x, axis=-1), 0.0)
    x = x + _L0_gnn_ref(h, edge_index, L0_gnn_weight, L0_gnn_w_ih, L0_gnn_w_hh, L0_gnn_b_ih, L0_gnn_b_hh)
    h = jnp.maximum(_layernorm(x, axis=-1), 0.0)
    x = x + _L1_gnn_ref(h, edge_index, edge_attr_96, L1_gnn_Wq, L1_gnn_bq, L1_gnn_Wk, L1_gnn_bk, L1_gnn_We, L1_gnn_be, L1_gnn_Wv, L1_gnn_bv)
    return x

_drawn_inputs = setup_inputs


def setup_inputs(seed=0):
    import zlib

    import numpy as np

    out = dict(_drawn_inputs(seed))
    spreads = {}
    factors = {'edge_attr_96': 2.719,
     'L0_gnn_b_ih': 7.102,
     'L0_gnn_b_hh': 8.0,
     'L1_gnn_bq': 8.0,
     'L1_gnn_Wk': 2.716,
     'L1_gnn_bk': 8.0,
     'L1_gnn_We': 2.737,
     'L1_gnn_be': 33.483}
    for name, (base, spread) in spreads.items():
        noise = np.random.default_rng([zlib.crc32(name.encode()), seed]).standard_normal(out[name].shape)
        drawn = base * np.exp(spread * noise) if base else spread * noise
        out[name] = jnp.asarray(drawn.astype(out[name].dtype))
    for name, factor in factors.items():
        out[name] = (out[name] * factor).astype(out[name].dtype)
    return out
```

```python
import numpy as np
import concourse.bass as bass
from concourse import mybir
from contextlib import ExitStack, contextmanager

N_NODES = 50000
N_EDGES = 12500
C = 96
ROUNDS = 3
HEADS = 8
HEAD_DIM = C // HEADS
P = 128
J = 3
U = P * J
G3 = 3 * C
DENSE_UNITS = -(-N_NODES // U)
LAST_DENSE_ROW = N_NODES - U
EDGE_UNITS = -(-N_EDGES // U)
E_TILES = EDGE_UNITS * J
E_PAD = E_TILES * P
MAP_COLS = -(-N_NODES // P)
M_COLS = C + HEADS
NO_NODE = N_NODES
SKIP = 1 << 16
EPS = 1e-5
RING = 4

F32 = mybir.dt.float32
I32 = mybir.dt.int32
ALU = mybir.AluOpType
ACTF = mybir.ActivationFunctionType
AXX = mybir.AxisListType.X


def wait(eng, sem, value):
    if isinstance(value, int) and value <= 0:
        return
    eng.wait_ge(sem, value)


def each_unit(eng, units, body):
    whole = units // RING
    for k in range(min(RING, units)):
        body(0, k)
    if whole > 2:
        with eng.Fori(1, whole - 1) as i:
            for k in range(RING):
                body(i, k)
    for u in range(max(RING, RING * (whole - 1)), units):
        body(u // RING, u % RING)


def ahead(i, k, d):
    return i + (k + d) // RING, (k + d) % RING


def exists(i, k, units):
    return not isinstance(i, int) or 0 <= RING * i + k < units


def build(nc, x, src_col, dst_col, dst_next_col, dst_row, edge_t, w_t, w_ih_t, w_hh_t, b_ih, b_hh,
          w_kv, b_kv, w_q, b_q, w_e, b_e, out):
    h_tab = [nc.dram_tensor(f"h{i}_table", (N_NODES + E_PAD, C), F32).ap() for i in (1, 2)] + [out]
    h0_edge = nc.dram_tensor("h0_edge", (E_PAD, C), F32).ap()
    x_edge = nc.dram_tensor("x_edge", (E_PAD, C), F32).ap()
    row_of = nc.dram_tensor("row_of", (P * MAP_COLS, 1), I32).ap()
    same_dram = nc.dram_tensor("same_dst", (EDGE_UNITS * P, U), F32).ap()
    goes_on_dram = nc.dram_tensor("goes_on", (EDGE_UNITS * P, U), F32).ap()

    def dense_rows(table, i, k):
        u = RING * i + k
        start = LAST_DENSE_ROW if isinstance(u, int) and u == DENSE_UNITS - 1 else u * U
        return table[bass.ds(start, U), :].rearrange("(p j) c -> p j c", p=P)

    def edge_rows(rows, i, k):
        return rows.rearrange("(p t) c -> p t c", p=P)[:, bass.ds((RING * i + k) * J, J), :]

    def mask_rows(rows, i, k):
        return rows[bass.ds((RING * i + k) * P, P), :]

    with ExitStack() as ctx:
        def sb(name, shape, dt=F32, stack=ctx):
            return stack.enter_context(nc.sbuf_tensor(name, shape, dt))

        def sem(name, stack=None):
            if stack is None:
                return ctx.enter_context(nc.semaphore(name))
            handle = nc.alloc_semaphore(name=name)
            taken.append(handle)
            return handle

        taken = []

        @contextmanager
        def phase():
            with ExitStack() as st:
                yield st
            nc.clear_and_free_semaphores(list(taken))
            taken.clear()
            nc.all_engine_barrier()

        ident = sb("ident", [P, P])
        w_h = sb("w_h", [C + 1, G3])
        w_f = [sb(f"w_f{i}", [C + 1, G3]) for i in range(ROUNDS)]
        w_kv_sb = sb("w_kv_sb", [C + 1, 2 * C])
        w_q_sb = sb("w_q_sb", [C + 1, C])
        w_e_sb = sb("w_e_sb", [C + 1, C])
        b_in = sb("b_in", [P, J, C])
        src_idx = sb("src_idx", [P, E_TILES], I32)
        dst_idx = sb("dst_idx", [P, E_TILES], I32)
        dst_safe = sb("dst_safe", [P, E_TILES], I32)
        scatter_idx = sb("scatter_idx", [P, E_TILES], I32)
        edge_row = sb("edge_row", [P, E_TILES], I32)
        src_row = sb("src_row", [P, E_TILES], I32)
        dst_row_idx = sb("dst_row_idx", [P, E_TILES], I32)
        src_h = sb("src_h", [P, E_TILES, C])
        dst_h = sb("dst_h", [P, E_TILES, C])

        got_x_src, got_x_dst = sem("got_x_src"), sem("got_x_dst")
        map_scattered, got_src_row, got_dst_row = sem("map_scattered"), sem("got_src_row"), sem("got_dst_row")
        got_h = [sem(f"got_h{i}") for i in range(ROUNDS)]
        got_x1_dst = sem("got_x1_dst")
        out_scattered = sem("out_scattered")
        ALL_TILES = 16 * E_TILES

        def gather(dest, table, idx, done):
            for t in range(E_TILES):
                yield lambda t=t: nc.gpsimd.indirect_dma_start(dest[:, t] if len(dest.shape) == 3 else dest[:, t:t + 1], None, table, bass.IndirectOffsetOnAxis(ap=idx[:, t:t + 1], axis=0)
                                             ).then_inc(done, 16)

        with phase() as st:
            w_t_sb = sb("w_t_sb", [C, ROUNDS, C], stack=st)
            w_ih_sb = sb("w_ih_sb", [C, G3], stack=st)
            b_ih_at = sb("b_ih_at", [C + 1, G3], stack=st)
            dst_next = sb("dst_next", [P, E_TILES], I32, stack=st)
            runs_on = sb("runs_on", [P, E_TILES], stack=st)
            iota_map = sb("iota_map", [P, MAP_COLS], I32, stack=st)
            ones = sb("ones", [P, P], stack=st)
            pw = st.enter_context(nc.psum_tensor("pw", [C, ROUNDS, 512], F32))
            loaded, map_set = sem("loaded", st), sem("map_set", st)
            ones_set, ident_set, iota_set, rows_set = (sem(n, st) for n in ("ones_set", "ident_set", "iota_set", "rows_set"))
            fused, fused_out, idx_step = sem("fused", st), sem("fused_out", st), sem("idx_step", st)
            LOADS = 17 + ROUNDS
            block = st.enter_context(nc.Block())

            @block.sync
            def _(sp):
                for dest, source in (
                    (w_t_sb[:], w_t.rearrange("i k m -> k i m")), (w_ih_sb[:], w_ih_t), (w_h[0:C, :], w_hh_t),
                    (w_h[C:C + 1, :], b_hh), (b_ih_at[C:C + 1, :], b_ih),
                    (w_kv_sb[0:C, :], w_kv), (w_kv_sb[C:C + 1, :], b_kv), (w_q_sb[0:C, :], w_q), (w_q_sb[C:C + 1, :], b_q),
                    (w_e_sb[0:C, :], w_e), (w_e_sb[C:C + 1, :], b_e),
                    (src_idx[:], src_col), (dst_idx[:], dst_col), (dst_next[:], dst_next_col),
                ):
                    sp.dma_start(dest, source).then_inc(loaded, 16)
                for j in range(J):
                    sp.dma_start(b_in[:, j, :], b_ih[0:1, 2 * C:G3].partition_broadcast(P)).then_inc(loaded, 16)
                for i in range(ROUNDS):
                    sp.dma_start(w_f[i][C:C + 1, 2 * C:G3], b_ih[0:1, 2 * C:G3]).then_inc(loaded, 16)
                sp.wait_ge(iota_set, 1)
                sp.dma_start(row_of.rearrange("(p c) o -> p (c o)", p=P), iota_map[:]).then_inc(map_set, 16)
                sp.wait_ge(loaded, 16 * LOADS)
                sp.wait_ge(map_set, 16)

            @block.gpsimd
            def _(pool):
                nc.gpsimd.iota(iota_map[:], [[1, MAP_COLS]], base=0, channel_multiplier=MAP_COLS).then_inc(iota_set, 1)
                nc.gpsimd.iota(edge_row[:], [[1, E_TILES]], base=N_NODES, channel_multiplier=E_TILES).then_inc(rows_set, 1)
                nc.gpsimd.memset(ones[:], 1.0).then_inc(ones_set, 1)
                pool.wait_ge(ones_set, 1)
                nc.gpsimd.affine_select(out=ident[:], in_=ones[:], compare_op=ALU.is_equal, fill=0.0, base=0,
                                        pattern=[[-1, P]], channel_multiplier=1).then_inc(ident_set, 1)
                pool.wait_ge(ident_set, 1)
                pool.wait_ge(rows_set, 1)

            @block.tensor
            def _(pe):
                pe.wait_ge(loaded, 16 * LOADS)
                for i in range(ROUNDS):
                    last = nc.tensor.matmul(pw[:, i, 0:G3], w_t_sb[:, i, :], w_ih_sb[:], start=True, stop=True)
                last.then_inc(fused, 1)

            @block.vector
            def _(dve):
                dve.wait_ge(loaded, 16 * LOADS)
                nc.vector.tensor_tensor(w_h[C:C + 1, C:G3], w_h[C:C + 1, C:G3], b_ih_at[C:C + 1, 0:2 * C], ALU.add)
                for i in range(ROUNDS):
                    nc.vector.memset(w_f[i][C:C + 1, 0:2 * C], 0.0)
                nc.vector.tensor_scalar(dst_safe[:], dst_idx[:], float(N_NODES - 1), None, ALU.min)
                nc.vector.tensor_tensor(runs_on[:], dst_idx[:], dst_next[:], ALU.is_equal).then_inc(idx_step, 1)
                dve.wait_ge(idx_step, 1)
                nc.vector.scalar_tensor_tensor(out=scatter_idx[:], in0=runs_on[:], scalar=float(SKIP), in1=dst_idx[:],
                                               op0=ALU.mult, op1=ALU.add)
                dve.wait_ge(fused, 1)
                for i in range(ROUNDS):
                    last = nc.vector.tensor_copy(w_f[i][0:C, :], pw[:, i, 0:G3])
                last.then_inc(fused_out, 1)
                dve.wait_ge(fused_out, 1)

        CHUNKS = 3
        CHUNK = E_TILES // CHUNKS
        STAT_STEPS = 2 + 2 * CHUNKS + 2

        def norm_stats(dve, rows_h, stat, scratch, step, squared, rooted, turn_no):
            n = STAT_STEPS * turn_no
            nc.vector.reduce_sum(stat[:, 0], rows_h[:], axis=AXX).then_inc(step, 1)
            dve.wait_ge(step, n + 1)
            nc.vector.tensor_scalar(stat[:, 1], stat[:, 0], 1.0 / C, None, ALU.mult).then_inc(step, 1)
            dve.wait_ge(step, n + 2)
            for c in range(CHUNKS):
                part = slice(c * CHUNK, (c + 1) * CHUNK)
                nc.vector.tensor_tensor(scratch[c][:], rows_h[:, part, :],
                                        stat[:, 1, part].unsqueeze(2).to_broadcast([P, CHUNK, C]), ALU.subtract).then_inc(step, 1)
            for c in range(CHUNKS):
                dve.wait_ge(squared, CHUNKS * turn_no + c + 1)
                nc.vector.reduce_sum(stat[:, 2, c * CHUNK:(c + 1) * CHUNK], scratch[c][:], axis=AXX).then_inc(step, 1)
            dve.wait_ge(step, n + 2 + 2 * CHUNKS)
            nc.vector.tensor_scalar(stat[:, 3], stat[:, 2], 1.0 / C, EPS, ALU.mult, ALU.add).then_inc(step, 1)
            dve.wait_ge(rooted, turn_no + 1)
            nc.vector.reciprocal(stat[:, 4], stat[:, 3]).then_inc(step, 1)
            dve.wait_ge(step, n + STAT_STEPS)

        def norm_stats_act(act, stat, scratch, step, squared, rooted, turn_no):
            n = STAT_STEPS * turn_no
            for c in range(CHUNKS):
                act.wait_ge(step, n + 2 + c + 1)
                nc.scalar.activation(scratch[c][:], scratch[c][:], ACTF.Square).then_inc(squared, 1)
            act.wait_ge(step, n + 2 + 2 * CHUNKS + 1)
            nc.scalar.activation(stat[:, 3], stat[:, 3], ACTF.Sqrt).then_inc(rooted, 1)

        def gru_phase(name, units, rows, h_source, h_dest, norm=False, fused_w=None, x_source=None, pool_work=None):
            edge = fused_w is not None
            with phase() as st:
                def ring(what, shape):
                    return [sb(f"{name}_{what}{k}", shape, stack=st) for k in range(RING)]

                def ring_sem(what):
                    return [sem(f"{name}_{what}{k}", st) for k in range(RING)]

                h_in = ring("h_in", [P, J, C])
                h = ring("h", [P, J, C]) if norm else h_in
                x_in = ring("x_in", [P, J, C]) if x_source is not None else None
                rz = ring("rz", [P, J, 2 * C])
                pre_n = ring("pre_n", [P, J, C])
                n = ring("n", [P, J, C])
                diff = ring("diff", [P, J, C])
                h_new = ring("h_new", [P, J, C])
                h_t = [sb(f"{name}_h_t{k}", [C + 1, U], stack=st) for k in range(2)]
                if norm:
                    stats, mean_var = ring("stats", [P, J, 6]), ring("mean_var", [P, J, 2])
                    rstd, shift = ring("rstd", [P, J]), ring("shift", [P, J])
                    minus_half = sb(f"{name}_minus_half", [P, J], stack=st)
                if edge:
                    v_in = ring("v_in", [P, J, C])
                    same = ring("same", [P, U])
                    goes_on = ring("goes_on", [P, U])
                    agg_t = [sb(f"{name}_agg_t{k}", [C + 1, U], stack=st) for k in range(2)]
                gates = [st.enter_context(nc.psum_tensor(f"{name}_gates{k}", [P, J, 512], F32)) for k in range(2)]
                turn = st.enter_context(nc.psum_tensor(f"{name}_turn", [P, 512], F32))
                agg_ps = st.enter_context(nc.psum_tensor(f"{name}_agg_ps", [P, 512], F32))

                in_loaded, stored = ring_sem("in_loaded"), ring_sem("stored")
                turned, h_t_ready, gates_done, rz_ready = (sem(f"{name}_{s}", st) for s in ("turned", "h_t_ready", "gates_done", "rz_ready"))
                mul_done, pre_ready, n_ready, diff_done, zdiff_done, blended, h_ready = (
                    sem(f"{name}_{s}", st) for s in ("mul_done", "pre_ready", "n_ready", "diff_done", "zdiff_done", "blended", "h_ready"))
                summed, carried, stats_seen, stats_made, moments, rstd_step, rstd_ready = (
                    sem(f"{name}_{s}", st) for s in ("summed", "carried", "stats_seen", "stats_made", "moments", "rstd_step", "rstd_ready"))
                ones_ready = sem(f"{name}_ones_ready", st)
                IN = 16 * (1 + (x_source is not None) + 3 * edge)
                block = st.enter_context(nc.Block())

                def load(sp, i, k):
                    if not exists(i, k, units):
                        return
                    done = in_loaded[k]
                    sp.dma_start(h_in[k][:], rows(h_source, i, k)).then_inc(done, 16)
                    if x_source is not None:
                        sp.dma_start(x_in[k][:], rows(x_source, i, k)).then_inc(done, 16)
                    if edge:
                        sp.dma_start(v_in[k][:], src_h[:, bass.ds((RING * i + k) * J, J), :]).then_inc(done, 16)
                        sp.dma_start(same[k][:], mask_rows(same_dram, i, k)).then_inc(done, 16)
                        sp.dma_start(goes_on[k][:], mask_rows(goes_on_dram, i, k)).then_inc(done, 16)

                @block.sync
                def _(sp):
                    for k in range(RING):
                        load(sp, 0, k)

                    def body(i, k):
                        u = RING * i + k
                        if norm:
                            sp.wait_ge(h_ready, u + 1)
                            load(sp, i + 1, k)
                        sp.wait_ge(blended, u + 1)
                        if isinstance(u, int) and u == units - 1 and not edge:
                            last = ahead(0, 0, u - 1)
                            sp.wait_ge(stored[last[1]], 16 * (last[0] + 1))
                        sp.dma_start(rows(h_dest, i, k), h_new[k][:]).then_inc(stored[k], 16)
                        if not norm:
                            load(sp, i + 1, k)

                    each_unit(sp, units, body)
                    for k in range(RING):
                        sp.wait_ge(stored[k], 16 * len(range(k, units, RING)))

                @block.gpsimd
                def _(pool):
                    todo = list(pool_work(pool)) if pool_work is not None else []
                    if norm:
                        nc.gpsimd.memset(minus_half[:], -0.5).then_inc(rstd_step, 1)
                        pool.wait_ge(rstd_step, 1)
                        for u in range(units):
                            k = u % RING
                            pool.wait_ge(moments, u + 1)
                            nc.gpsimd.tensor_scalar(rstd[k][:], mean_var[k][:, :, 1], EPS, None, ALU.add).then_inc(rstd_step, 1)
                            pool.wait_ge(rstd_step, 3 * u + 2)
                            nc.gpsimd.tensor_tensor(rstd[k][:], rstd[k][:], minus_half[:], ALU.pow).then_inc(rstd_step, 1)
                            pool.wait_ge(rstd_step, 3 * u + 3)
                            nc.gpsimd.tensor_tensor(shift[k][:], mean_var[k][:, :, 0], rstd[k][:], ALU.mult).then_inc(rstd_step, 1)
                            pool.wait_ge(rstd_step, 3 * u + 4)
                            nc.gpsimd.tensor_scalar(shift[k][:], shift[k][:], -1.0, None, ALU.mult).then_inc(rstd_ready, 1)
                            for task in todo[len(todo) * u // units:len(todo) * (u + 1) // units]:
                                task()
                    else:
                        for task in todo:
                            task()

                @block.tensor
                def _(pe):
                    def turn_unit(i, k):
                        u = RING * i + k
                        if norm:
                            pe.wait_ge(h_ready, u + 1)
                        else:
                            pe.wait_ge(in_loaded[k], IN * (i + 1))
                        for j in range(J):
                            last = nc.tensor.transpose(turn[0:C, P * j:P * (j + 1)], h[k][:, j, :], ident[:])
                        last.then_inc(turned, 1)
                        if edge:
                            for j in range(J):
                                last = nc.tensor.matmul(agg_ps[0:C, P * j:P * (j + 1)], v_in[k][:, j, :],
                                                        same[k][:, P * j:P * (j + 1)], start=True, stop=True)
                            last.then_inc(summed, 1)

                    turn_unit(0, 0)
                    pe.wait_ge(ones_ready, 1)

                    def body(i, k):
                        u, par = RING * i + k, k % 2
                        pe.wait_ge(h_t_ready, u + 1)
                        if edge:
                            pe.wait_ge(carried, u + 1)
                        wait(pe, pre_ready if edge else mul_done, u - 1)
                        for j in range(J):
                            last = nc.tensor.matmul(gates[par][:, j, 0:G3], h_t[par][:, P * j:P * (j + 1)], w_h[:],
                                                    start=True, stop=True)
                            if edge:
                                last = nc.tensor.matmul(gates[par][:, j, C:C + G3], agg_t[par][:, P * j:P * (j + 1)],
                                                        fused_w[:], start=False, stop=True, skip_group_check=True)
                        last.then_inc(gates_done, 1)
                        nxt = ahead(i, k, 1)
                        if exists(*nxt, units):
                            turn_unit(*nxt)

                    each_unit(pe, units, body)

                @block.scalar
                def _(act):
                    def turned_out(i, k):
                        u = RING * i + k
                        act.wait_ge(turned, u + 1)
                        nc.scalar.copy(h_t[k % 2][0:C, :], turn[0:C, 0:U]).then_inc(h_t_ready, 1)

                    def tanh(i, k):
                        u = RING * i + k
                        act.wait_ge(pre_ready, u + 1)
                        nc.scalar.activation(n[k][:], pre_n[k][:], ACTF.Tanh).then_inc(n_ready, 1)

                    def norm_out(i, k):
                        u = RING * i + k
                        act.wait_ge(rstd_ready, u + 1)
                        act.wait_ge(in_loaded[k], IN * (i + 1))
                        wait(act, blended, u - RING + 1)
                        for j in range(J):
                            last = nc.scalar.activation(h[k][:, j, :], h_in[k][:, j, :], ACTF.Relu,
                                                        bias=shift[k][:, j:j + 1], scale=rstd[k][:, j:j + 1])
                        last.then_inc(h_ready, 1)

                    if norm:
                        norm_out(0, 0)
                        norm_out(0, 1)
                    turned_out(0, 0)

                    def body(i, k):
                        u = RING * i + k
                        act.wait_ge(gates_done, u + 1)
                        wait(act, blended, u - RING + 1)
                        nc.scalar.activation(rz[k][:], gates[k % 2][:, :, C:G3], ACTF.Sigmoid).then_inc(rz_ready, 1)
                        prev = ahead(i, k, -1)
                        if exists(*prev, units):
                            tanh(*prev)
                        nxt = ahead(i, k, 1)
                        if exists(*nxt, units):
                            turned_out(*nxt)
                        nxt = ahead(i, k, 2)
                        if norm and exists(*nxt, units):
                            norm_out(*nxt)

                    each_unit(act, units, body)
                    tanh(*ahead(0, 0, units - 1))

                @block.vector
                def _(dve):
                    for par in range(2):
                        last = nc.vector.memset(h_t[par][C:C + 1, :], 1.0)
                        if edge:
                            nc.vector.memset(agg_t[par][C:C + 1, :], 1.0)
                            last = nc.vector.memset(agg_t[par][0:C, :], 0.0)
                    last.then_inc(ones_ready, 1)
                    dve.wait_ge(ones_ready, 1)

                    def moments_of(i, k):
                        u = RING * i + k
                        dve.wait_ge(in_loaded[k], IN * (i + 1))
                        wait(dve, rstd_ready, u - RING + 1)
                        for j in range(J):
                            last = nc.vector.bn_stats(stats[k][:, j, :], h_in[k][:, j, :])
                        last.then_inc(stats_made, 1)
                        dve.wait_ge(stats_made, u + 1)
                        dve.sem_inc(stats_seen, 1)
                        for j in range(J):
                            last = nc.vector.bn_aggr(mean_var[k][:, j, :], stats[k][:, j, :])
                        last.then_inc(moments, 1)

                    def carry(i, k):
                        u, par = RING * i + k, k % 2
                        dve.wait_ge(summed, u + 1)
                        for j in range(J):
                            before = agg_t[par][0:C, P * j - 1:P * j] if j else agg_t[1 - par][0:C, U - 1:U]
                            nc.vector.scalar_tensor_tensor(
                                out=agg_t[par][0:C, P * j:P * (j + 1)], in0=goes_on[k][0:C, P * j:P * (j + 1)], scalar=before,
                                in1=agg_ps[0:C, P * j:P * (j + 1)], op0=ALU.mult, op1=ALU.add).then_inc(
                                    carried if j == J - 1 else diff_carry, 1)
                            if j == J - 1:
                                dve.wait_ge(carried, u + 1)
                            else:
                                dve.wait_ge(diff_carry, (J - 1) * u + j + 1)

                    def blend(i, k):
                        u = RING * i + k
                        dve.wait_ge(n_ready, u + 1)
                        nc.vector.tensor_tensor(diff[k][:], h[k][:], n[k][:], ALU.subtract).then_inc(diff_done, 1)
                        dve.wait_ge(diff_done, u + 1)
                        nc.vector.tensor_tensor(diff[k][:], rz[k][:, :, C:2 * C], diff[k][:], ALU.mult).then_inc(zdiff_done, 1)
                        dve.wait_ge(zdiff_done, (1 + (x_source is not None)) * u + 1)
                        if x_source is not None:
                            dve.wait_ge(in_loaded[k], IN * (i + 1))
                            nc.vector.tensor_tensor(diff[k][:], x_in[k][:], diff[k][:], ALU.add).then_inc(zdiff_done, 1)
                            dve.wait_ge(zdiff_done, 2 * u + 2)
                        wait(dve, stored[k], 16 * i)
                        nc.vector.tensor_tensor(h_new[k][:], n[k][:], diff[k][:], ALU.add).then_inc(blended, 1)

                    if norm:
                        for k in range(3):
                            moments_of(0, k)
                    if edge:
                        carry(0, 0)

                    def body(i, k):
                        u, par = RING * i + k, k % 2
                        dve.wait_ge(rz_ready, u + 1)
                        nc.vector.tensor_tensor(pre_n[k][:], gates[par][:, :, 0:C], rz[k][:, :, 0:C], ALU.mult).then_inc(mul_done, 1)
                        dve.wait_ge(mul_done, u + 1)
                        bias = gates[par][:, :, G3:G3 + C] if edge else b_in[:]
                        nc.vector.tensor_tensor(pre_n[k][:], bias, pre_n[k][:], ALU.add).then_inc(pre_ready, 1)
                        prev = ahead(i, k, -1)
                        if exists(*prev, units):
                            blend(*prev)
                        nxt = ahead(i, k, 3)
                        if norm and exists(*nxt, units):
                            moments_of(*nxt)
                        nxt = ahead(i, k, 1)
                        if edge and exists(*nxt, units):
                            carry(*nxt)

                    each_unit(dve, units, body)
                    blend(*ahead(0, 0, units - 1))
                    dve.wait_ge(blended, units)

        diff_carry = None
        edge_part = lambda table: table[N_NODES:N_NODES + E_PAD, :]

        def pool_round1(pool):
            yield from gather(src_h, x, src_idx, got_x_src)
            yield from gather(dst_h, x, dst_safe, got_x_dst)
            for t in range(E_TILES):
                yield lambda t=t: nc.gpsimd.indirect_dma_start(row_of[:, :], bass.IndirectOffsetOnAxis(ap=scatter_idx[:, t:t + 1], axis=0),
                                             edge_row[:, t:t + 1], None, bounds_check=N_NODES - 1, oob_is_err=False
                                             ).then_inc(map_scattered, 16)
            yield lambda: pool.wait_ge(map_scattered, ALL_TILES)

        gru_phase("all1", DENSE_UNITS, dense_rows, x, h_tab[0], norm=True, pool_work=pool_round1)

        with phase() as st:
            stat = [sb(f"prep_stat{n}", [P, 5, E_TILES], stack=st) for n in range(2)]
            scratch = [sb(f"prep_scratch{c}", [P, CHUNK, C], stack=st) for c in range(CHUNKS)]
            dst_all = [sb(f"dst_all{k}", [P, U + 1], I32, stack=st) for k in range(RING)]
            same_o = [sb(f"same_o{k}", [P, U], stack=st) for k in range(RING)]
            goes_o = [sb(f"goes_o{k}", [P, U], stack=st) for k in range(RING)]
            dst_loaded = [sem(f"dst_loaded{k}", st) for k in range(RING)]
            masks_stored = [sem(f"masks_stored{k}", st) for k in range(RING)]
            x_saved, h0_saved, prep_step, masks_made, squared, rooted, centered, normed = (
                sem(s, st) for s in ("x_saved", "h0_saved", "prep_step", "masks_made", "prep_squared", "prep_rooted", "prep_centered", "prep_normed"))
            block = st.enter_context(nc.Block())

            @block.sync
            def _(sp):
                def load(i, k):
                    if exists(i, k, EDGE_UNITS):
                        sp.dma_start(dst_all[k][:], dst_row[0:1, bass.ds((RING * i + k) * U, U + 1)].partition_broadcast(P)
                                     ).then_inc(dst_loaded[k], 16)

                sp.wait_ge(got_x_dst, ALL_TILES)
                sp.dma_start(x_edge.rearrange("(p t) c -> p t c", p=P), dst_h[:]).then_inc(x_saved, 16)
                for k in range(RING):
                    load(0, k)

                def body(i, k):
                    u = RING * i + k
                    sp.wait_ge(masks_made, 2 * (u + 1))
                    sp.dma_start(mask_rows(same_dram, i, k), same_o[k][:]).then_inc(masks_stored[k], 16)
                    sp.dma_start(mask_rows(goes_on_dram, i, k), goes_o[k][:]).then_inc(masks_stored[k], 16)
                    load(i + 1, k)

                each_unit(sp, EDGE_UNITS, body)
                sp.wait_ge(normed, 2)
                sp.dma_start(h0_edge.rearrange("(p t) c -> p t c", p=P), dst_h[:]).then_inc(h0_saved, 16)
                sp.wait_ge(h0_saved, 16)
                for k in range(RING):
                    sp.wait_ge(masks_stored[k], 32 * len(range(k, EDGE_UNITS, RING)))

            @block.vector
            def _(dve):
                def body(i, k):
                    u = RING * i + k
                    dve.wait_ge(dst_loaded[k], 16 * (i + 1))
                    if not (isinstance(i, int) and i == 0):
                        dve.wait_ge(masks_stored[k], 32 * i)
                    here = dst_all[k][:, 1:U + 1].rearrange("p (j e) -> p j e", j=J)
                    before = dst_all[k][:, 0:U].rearrange("p (j e) -> p j e", j=J)[:, :, 0:1]
                    mine = dst_idx[:, bass.ds(u * J, J)].unsqueeze(2)
                    nc.vector.tensor_tensor(same_o[k][:].rearrange("p (j e) -> p j e", j=J), here,
                                            mine.to_broadcast([P, J, P]), ALU.is_equal).then_inc(masks_made, 1)
                    nc.vector.tensor_tensor(goes_o[k][:].rearrange("p (j e) -> p j e", j=J), here,
                                            before.to_broadcast([P, J, P]), ALU.is_equal).then_inc(masks_made, 1)

                each_unit(dve, EDGE_UNITS, body)
                dve.wait_ge(got_x_src, ALL_TILES)
                dve.wait_ge(x_saved, 16)
                for n, rows_h in enumerate((src_h, dst_h)):
                    norm_stats(dve, rows_h, stat[n], scratch, prep_step, squared, rooted, n)
                    nc.vector.tensor_tensor(rows_h[:], rows_h[:], stat[n][:, 1].unsqueeze(2).to_broadcast([P, E_TILES, C]),
                                            ALU.subtract).then_inc(centered, 1)
                    dve.wait_ge(centered, n + 1)
                    nc.vector.scalar_tensor_tensor(out=rows_h[:], in0=rows_h[:], scalar=0.0,
                                                   in1=stat[n][:, 4].unsqueeze(2).to_broadcast([P, E_TILES, C]),
                                                   op0=ALU.max, op1=ALU.mult).then_inc(normed, 1)

            @block.scalar
            def _(act):
                for n in range(2):
                    norm_stats_act(act, stat[n], scratch, prep_step, squared, rooted, n)

            @block.gpsimd
            def _(pool):
                for task in gather(src_row, row_of[:, :], src_idx, got_src_row):
                    task()

        diff_carry = sem("tile_carried1")
        gru_phase("edge1", EDGE_UNITS, edge_rows, h0_edge, edge_part(h_tab[0]), fused_w=w_f[0])

        def pool_round2(pool):
            yield lambda: pool.wait_ge(got_src_row, ALL_TILES)
            yield from gather(src_h, h_tab[0], src_row, got_h[0])
            yield lambda: pool.wait_ge(got_h[0], ALL_TILES)
            yield from gather(dst_row_idx, row_of[:, :], dst_safe, got_dst_row)
            yield lambda: pool.wait_ge(got_dst_row, ALL_TILES)

        gru_phase("all2", DENSE_UNITS, dense_rows, h_tab[0], h_tab[1], pool_work=pool_round2)
        diff_carry = sem("tile_carried2")
        gru_phase("edge2", EDGE_UNITS, edge_rows, edge_part(h_tab[0]), edge_part(h_tab[1]), fused_w=w_f[1])

        def pool_round3(pool):
            yield from gather(src_h, h_tab[1], src_row, got_h[1])
            yield lambda: pool.wait_ge(got_h[1], ALL_TILES)

        gru_phase("all3", DENSE_UNITS, dense_rows, h_tab[1], out, x_source=x, pool_work=pool_round3)
        diff_carry = sem("tile_carried3")
        gru_phase("edge3", EDGE_UNITS, edge_rows, edge_part(h_tab[1]), edge_part(out), fused_w=w_f[2], x_source=x_edge)

        with phase() as st:
            def two(what, shape):
                return [sb(f"att_{what}{k}", shape, stack=st) for k in range(2)]

            def ring(what, shape):
                return [sb(f"att_{what}{k}", shape, stack=st) for k in range(RING)]

            stat = [sb(f"att_stat{n}", [P, 5, E_TILES], stack=st) for n in range(2)]
            scratch = [sb(f"att_scratch{c}", [P, CHUNK, C], stack=st) for c in range(CHUNKS)]
            centered_row = [sb(f"att_centered{n}", [P, J, C], stack=st) for n in range(2)]
            same, goes_on, e_t = ring("same", [P, U]), ring("goes_on", [P, U]), ring("e_t", [C + 1, U])
            hs, hd = two("hs", [P, J, C]), two("hd", [P, J, C])
            hs_t, hd_t = two("hs_t", [C + 1, U]), two("hd_t", [C + 1, U])
            kq, score = sb("att_kq", [P, J, C], stack=st), sb("att_score", [P, J, HEADS], stack=st)
            msg = two("msg", [P, J, M_COLS])
            sum_t = two("sum_t", [M_COLS, U])
            z_inv, mix = sb("att_z_inv", [P, J, HEADS], stack=st), sb("att_mix", [P, J, C], stack=st)
            proj = st.enter_context(nc.psum_tensor("att_proj", [P, J, 512], F32))
            turn_s = st.enter_context(nc.psum_tensor("att_turn_s", [P, 512], F32))
            turn_d = st.enter_context(nc.psum_tensor("att_turn_d", [P, 512], F32))
            sums = st.enter_context(nc.psum_tensor("att_sums", [P, 512], F32))
            back = st.enter_context(nc.psum_tensor("att_back", [P, 512], F32))
            in_loaded = [sem(f"att_in_loaded{k}", st) for k in range(RING)]
            (stat_step, squared, rooted, centered, normed, turned, h_t_ready, projected, score_step, weights_ready, msg_ready, summed, carried,
             back_done, mix_step, mixed, ones_ready) = (
                sem(f"att_{s}", st) for s in ("stat_step", "squared", "rooted", "centered", "normed", "turned", "h_t_ready", "projected", "score_step", "weights_ready",
                                              "msg_ready", "summed", "carried", "back_done", "mix_step", "mixed", "ones_ready"))
            block = st.enter_context(nc.Block())

            @block.sync
            def _(sp):
                def load(i, k):
                    if exists(i, k, EDGE_UNITS):
                        u = RING * i + k
                        sp.dma_start(same[k][:], mask_rows(same_dram, i, k)).then_inc(in_loaded[k], 16)
                        sp.dma_start(goes_on[k][:], mask_rows(goes_on_dram, i, k)).then_inc(in_loaded[k], 16)
                        sp.dma_start(e_t[k][0:C, :], edge_t[:, bass.ds(u * U, U)]).then_inc(in_loaded[k], 16)

                for k in range(RING):
                    load(0, k)

                def body(i, k):
                    sp.wait_ge(carried, J * (RING * i + k + 1))
                    load(i + 1, k)

                each_unit(sp, EDGE_UNITS, body)

            @block.gpsimd
            def _(pool):
                for task in [*gather(src_h, out, src_row, got_h[2]), *gather(dst_h, out, dst_row_idx, got_x1_dst)]:
                    task()
                pool.wait_ge(got_h[2], ALL_TILES)
                pool.wait_ge(got_x1_dst, ALL_TILES)
                for t in range(E_TILES):
                    if t % J == 0:
                        pool.wait_ge(mixed, t // J + 1)
                    nc.gpsimd.indirect_dma_start(out, bass.IndirectOffsetOnAxis(ap=scatter_idx[:, t:t + 1], axis=0),
                                                 dst_h[:, t], None, bounds_check=N_NODES - 1, oob_is_err=False
                                                 ).then_inc(out_scattered, 16)
                pool.wait_ge(out_scattered, ALL_TILES)

            @block.tensor
            def _(pe):
                pe.wait_ge(ones_ready, 1)

                def turn_unit(i, k):
                    u = RING * i + k
                    pe.wait_ge(normed, 2 * (u + 1))
                    for dest, source in ((turn_s, hs[k % 2]), (turn_d, hd[k % 2])):
                        for j in range(J):
                            last = nc.tensor.transpose(dest[0:C, P * j:P * (j + 1)], source[:, j, :], ident[:])
                    last.then_inc(turned, 1)

                turn_unit(0, 0)

                def body(i, k):
                    u, par = RING * i + k, k % 2
                    pe.wait_ge(h_t_ready, 2 * (u + 1))
                    pe.wait_ge(in_loaded[k], 48 * (i + 1))
                    wait(pe, msg_ready, u)
                    for j in range(J):
                        cols = slice(P * j, P * (j + 1))
                        nc.tensor.matmul(proj[:, j, 0:2 * C], hs_t[par][:, cols], w_kv_sb[:], start=True, stop=True)
                        nc.tensor.matmul(proj[:, j, 2 * C:3 * C], hd_t[par][:, cols], w_q_sb[:], start=True, stop=True)
                        last = nc.tensor.matmul(proj[:, j, 3 * C:4 * C], e_t[k][:, cols], w_e_sb[:], start=True, stop=True)
                    last.then_inc(projected, 1)
                    nxt = ahead(i, k, 1)
                    if exists(*nxt, EDGE_UNITS):
                        turn_unit(*nxt)
                    pe.wait_ge(msg_ready, u + 1)
                    for j in range(J):
                        last = nc.tensor.matmul(sums[0:M_COLS, P * j:P * (j + 1)], msg[par][:, j, :], same[k][:, P * j:P * (j + 1)],
                                                start=True, stop=True)
                    last.then_inc(summed, 1)
                    pe.wait_ge(carried, J * (u + 1))
                    wait(pe, mixed, u)
                    for j in range(J):
                        last = nc.tensor.transpose(back[:, M_COLS * j:M_COLS * (j + 1)], sum_t[par][:, P * j:P * (j + 1)],
                                                   ident[0:M_COLS, 0:M_COLS])
                    last.then_inc(back_done, 1)

                each_unit(pe, EDGE_UNITS, body)

            @block.scalar
            def _(act):
                def turned_out(i, k):
                    act.wait_ge(turned, RING * i + k + 1)
                    nc.scalar.copy(hs_t[k % 2][0:C, :], turn_s[0:C, 0:U]).then_inc(h_t_ready, 1)
                    nc.scalar.copy(hd_t[k % 2][0:C, :], turn_d[0:C, 0:U]).then_inc(h_t_ready, 1)

                for n in range(2):
                    norm_stats_act(act, stat[n], scratch, stat_step, squared, rooted, n)
                turned_out(0, 0)

                def body(i, k):
                    u = RING * i + k
                    nxt = ahead(i, k, 1)
                    if exists(*nxt, EDGE_UNITS):
                        wait(act, projected, u)
                        turned_out(*nxt)
                    act.wait_ge(score_step, 5 * (u + 1))
                    wait(act, summed, u - 1)
                    nc.scalar.activation(msg[k % 2][:, :, C:M_COLS], score[:], ACTF.Exp).then_inc(weights_ready, 1)

                each_unit(act, EDGE_UNITS, body)

            @block.vector
            def _(dve):
                for par in range(2):
                    nc.vector.memset(hs_t[par][C:C + 1, :], 1.0)
                    nc.vector.memset(hd_t[par][C:C + 1, :], 1.0)
                    nc.vector.memset(sum_t[par][:], 0.0)
                for k in range(RING):
                    last = nc.vector.memset(e_t[k][C:C + 1, :], 1.0)
                last.then_inc(ones_ready, 1)
                dve.wait_ge(ones_ready, 1)
                dve.wait_ge(got_h[2], ALL_TILES)
                norm_stats(dve, src_h, stat[0], scratch, stat_step, squared, rooted, 0)
                dve.wait_ge(got_x1_dst, ALL_TILES)
                norm_stats(dve, dst_h, stat[1], scratch, stat_step, squared, rooted, 1)

                def norm_unit(i, k):
                    u = RING * i + k
                    wait(dve, turned, u - 1)
                    for n, (rows_h, dest) in enumerate(((src_h, hs), (dst_h, hd))):
                        tiles = bass.ds(u * J, J)
                        nc.vector.tensor_tensor(centered_row[n][:], rows_h[:, tiles, :],
                                                stat[n][:, 1, tiles].unsqueeze(2).to_broadcast([P, J, C]), ALU.subtract).then_inc(centered, 1)
                        dve.wait_ge(centered, 2 * u + n + 1)
                        nc.vector.scalar_tensor_tensor(out=dest[k % 2][:], in0=centered_row[n][:], scalar=0.0,
                                                       in1=stat[n][:, 4, tiles].unsqueeze(2).to_broadcast([P, J, C]),
                                                       op0=ALU.max, op1=ALU.mult).then_inc(normed, 1)

                norm_unit(0, 0)

                def body(i, k):
                    u, par = RING * i + k, k % 2
                    nxt = ahead(i, k, 1)
                    if exists(*nxt, EDGE_UNITS):
                        norm_unit(*nxt)
                    dve.wait_ge(projected, u + 1)
                    wait(dve, weights_ready, u)
                    nc.vector.tensor_copy(kq[:], proj[:, :, 2 * C:3 * C]).then_inc(score_step, 1)
                    dve.wait_ge(score_step, 5 * u + 1)
                    nc.vector.tensor_tensor(kq[:], proj[:, :, 0:C], kq[:], ALU.mult).then_inc(score_step, 1)
                    dve.wait_ge(score_step, 5 * u + 2)
                    nc.vector.tensor_tensor(kq[:], proj[:, :, 3 * C:4 * C], kq[:], ALU.mult).then_inc(score_step, 1)
                    dve.wait_ge(score_step, 5 * u + 3)
                    nc.vector.reduce_sum(score[:], kq[:].rearrange("p j (h d) -> p j h d", h=HEADS), axis=AXX).then_inc(score_step, 1)
                    dve.wait_ge(score_step, 5 * u + 4)
                    nc.vector.tensor_scalar(score[:], score[:], float(HEAD_DIM) ** -0.5, 5.0, ALU.mult, ALU.min).then_inc(mix_step, 1)
                    dve.wait_ge(mix_step, 4 * u + 1)
                    nc.vector.tensor_scalar(score[:], score[:], -5.0, None, ALU.max).then_inc(score_step, 1)
                    dve.wait_ge(weights_ready, u + 1)
                    weights = msg[par][:, :, C:M_COLS].unsqueeze(3).to_broadcast([P, J, HEADS, HEAD_DIM])
                    nc.vector.tensor_tensor(msg[par][:, :, 0:C].rearrange("p j (h d) -> p j h d", h=HEADS),
                                            proj[:, :, C:2 * C].rearrange("p j (h d) -> p j h d", h=HEADS), weights,
                                            ALU.mult).then_inc(msg_ready, 1)
                    dve.wait_ge(summed, u + 1)
                    for j in range(J):
                        before = sum_t[par][:, P * j - 1:P * j] if j else sum_t[1 - par][:, U - 1:U]
                        nc.vector.scalar_tensor_tensor(
                            out=sum_t[par][:, P * j:P * (j + 1)], in0=goes_on[k][0:M_COLS, P * j:P * (j + 1)], scalar=before,
                            in1=sums[0:M_COLS, P * j:P * (j + 1)], op0=ALU.mult, op1=ALU.add).then_inc(carried, 1)
                        dve.wait_ge(carried, J * u + j + 1)
                    dve.wait_ge(back_done, u + 1)
                    rows_b = back[:, 0:J * M_COLS].rearrange("p (j m) -> p j m", j=J)
                    nc.vector.tensor_scalar(z_inv[:], rows_b[:, :, C:M_COLS], 1e-6, None, ALU.add).then_inc(mix_step, 1)
                    dve.wait_ge(mix_step, 4 * u + 2)
                    nc.vector.reciprocal(z_inv[:], z_inv[:]).then_inc(mix_step, 1)
                    dve.wait_ge(mix_step, 4 * u + 3)
                    nc.vector.tensor_tensor(mix[:].rearrange("p j (h d) -> p j h d", h=HEADS),
                                            rows_b[:, :, 0:C].rearrange("p j (h d) -> p j h d", h=HEADS),
                                            z_inv[:].unsqueeze(3).to_broadcast([P, J, HEADS, HEAD_DIM]), ALU.mult).then_inc(mix_step, 1)
                    dve.wait_ge(mix_step, 4 * u + 4)
                    mine = dst_h[:, bass.ds(u * J, J), :]
                    nc.vector.tensor_tensor(mine, mine, mix[:], ALU.add).then_inc(mixed, 1)

                each_unit(dve, EDGE_UNITS, body)
    return nc


def kernel(x, src, dst, edge_attr_96, L0_gnn_weight, L0_gnn_w_ih, L0_gnn_w_hh, L0_gnn_b_ih, L0_gnn_b_hh,
           L1_gnn_Wq, L1_gnn_bq, L1_gnn_Wk, L1_gnn_bk, L1_gnn_We, L1_gnn_be, L1_gnn_Wv, L1_gnn_bv):
    import numpy as _np
    import concourse.bacc as _bacc
    from concourse import mybir as _mybir
    from concourse.bass_utils import run_bass_kernel_spmd as _run

    a = _np.asarray
    src, dst, edge = a(src), a(dst), a(edge_attr_96)
    w_hh, b_hh, b_ih = a(L0_gnn_w_hh), a(L0_gnn_b_hh), a(L0_gnn_b_ih)
    pad = E_PAD - N_EDGES

    def columns(v):
        return _np.ascontiguousarray(v.reshape(E_TILES, P).T)

    def n_first(v):
        return _np.concatenate([v[2 * C:], v[:2 * C]], 0)

    src_p = _np.concatenate([src, _np.zeros(pad, src.dtype)])
    dst_p = _np.concatenate([dst, _np.full(pad + 1, NO_NODE, dst.dtype)])
    arrays = {
        "x": a(x),
        "src_col": columns(src_p),
        "dst_col": columns(dst_p[:-1]),
        "dst_next_col": columns(dst_p[1:]),
        "dst_row": _np.concatenate([_np.full(1, -1, dst.dtype), dst_p[:-1]])[None, :],
        "edge_t": _np.concatenate([edge, _np.zeros((pad, C), edge.dtype)], 0).T,
        "w_t": a(L0_gnn_weight).transpose(0, 2, 1),
        "w_ih_t": a(L0_gnn_w_ih).T,
        "w_hh_t": n_first(w_hh).T,
        "b_ih": b_ih[None, :],
        "b_hh": n_first(b_hh)[None, :],
        "w_kv": _np.concatenate([a(L1_gnn_Wk), a(L1_gnn_Wv)], 1),
        "b_kv": _np.concatenate([a(L1_gnn_bk), a(L1_gnn_bv)])[None, :],
        "w_q": a(L1_gnn_Wq), "b_q": a(L1_gnn_bq)[None, :],
        "w_e": a(L1_gnn_We), "b_e": a(L1_gnn_be)[None, :],
    }
    nc = _bacc.Bacc("TRN2", target_bir_lowering=False, num_devices=1)
    feed, args = {}, []
    for name, v in arrays.items():
        v = _np.ascontiguousarray(v)
        feed[f"in_{name}"] = v
        args.append(nc.dram_tensor(f"in_{name}", v.shape, _mybir.dt.from_np(v.dtype), kind="ExternalInput").ap())
    args.append(nc.dram_tensor("out", (N_NODES + E_PAD, C), F32, kind="ExternalOutput").ap())
    build(nc, *args)
    r = _run(nc, [feed], core_ids=[0])
    return r.results[0]["out"][:N_NODES]
```

```python
import numpy as np
import concourse.bass as bass
from concourse import mybir
from contextlib import ExitStack, contextmanager

N_NODES = 50000
N_EDGES = 12500
C = 96
ROUNDS = 3
HEADS = 8
HEAD_DIM = C // HEADS
P = 128
J = 3
U = P * J
G3 = 3 * C
DENSE_UNITS = -(-N_NODES // U)
LAST_DENSE_ROW = N_NODES - U
EDGE_UNITS = -(-N_EDGES // U)
E_TILES = EDGE_UNITS * J
E_PAD = E_TILES * P
MAP_COLS = -(-N_NODES // P)
M_COLS = C + HEADS
NO_NODE = N_NODES
SKIP = 1 << 16
EPS = 1e-5
RING = 6

F32 = mybir.dt.float32
I32 = mybir.dt.int32
ALU = mybir.AluOpType
ACTF = mybir.ActivationFunctionType
AXX = mybir.AxisListType.X


def wait(eng, sem, value):
    if isinstance(value, int) and value <= 0:
        return
    eng.wait_ge(sem, value)


def each_unit(eng, units, body):
    whole = units // RING
    for k in range(min(RING, units)):
        body(0, k)
    if whole > 2:
        with eng.Fori(1, whole - 1) as i:
            for k in range(RING):
                body(i, k)
    for u in range(max(RING, RING * (whole - 1)), units):
        body(u // RING, u % RING)


def ahead(i, k, d):
    return i + (k + d) // RING, (k + d) % RING


def exists(i, k, units):
    return not isinstance(i, int) or 0 <= RING * i + k < units


def build(nc, x, src_col, dst_col, dst_next_col, dst_row, edge_t, w_t, w_ih_t, w_hh_t, b_ih, b_hh,
          w_kv, b_kv, w_q, b_q, w_e, b_e, out):
    h_tab = [nc.dram_tensor(f"h{i}_table", (N_NODES + E_PAD, C), F32).ap() for i in (1, 2)] + [out]
    x1_edge = nc.dram_tensor("x1_edge", (E_PAD, C), F32).ap()
    x_edge = nc.dram_tensor("x_edge", (E_PAD, C), F32).ap()
    row_of = nc.dram_tensor("row_of", (P * MAP_COLS, 1), I32).ap()
    same_dram = nc.dram_tensor("same_dst", (EDGE_UNITS * P, U), F32).ap()
    goes_on_dram = nc.dram_tensor("goes_on", (EDGE_UNITS * P, U), F32).ap()

    def dense_rows(table, first=0):
        def rows(i, k):
            u = RING * i + k
            start = LAST_DENSE_ROW if isinstance(u, int) and first + u == DENSE_UNITS - 1 else (first + u) * U
            return table[bass.ds(start, U), :].rearrange("(p j) c -> p j c", p=P)
        return rows

    def edge_rows(array):
        return lambda i, k: array.rearrange("(p t) c -> p t c", p=P)[:, bass.ds((RING * i + k) * J, J), :]

    def edge_part(table):
        return edge_rows(table[N_NODES:N_NODES + E_PAD, :])

    def mask_rows(rows, i, k):
        return rows[bass.ds((RING * i + k) * P, P), :]

    with ExitStack() as ctx:
        def sb(name, shape, dt=F32, stack=ctx):
            return stack.enter_context(nc.sbuf_tensor(name, shape, dt))

        def sem(name, stack=None):
            if stack is None:
                return ctx.enter_context(nc.semaphore(name))
            handle = nc.alloc_semaphore(name=name)
            taken.append(handle)
            return handle

        taken = []

        @contextmanager
        def phase():
            with ExitStack() as st:
                yield st
            nc.clear_and_free_semaphores(list(taken))
            taken.clear()
            nc.all_engine_barrier()

        ident = sb("ident", [P, P])
        w_h = sb("w_h", [C + 1, G3])
        w_f = [sb(f"w_f{i}", [C + 1, G3]) for i in range(ROUNDS)]
        w_kv_sb = sb("w_kv_sb", [C + 1, 2 * C])
        w_q_sb = sb("w_q_sb", [C + 1, C])
        w_e_sb = sb("w_e_sb", [C + 1, C])
        b_in = sb("b_in", [P, J, C])
        src_idx = sb("src_idx", [P, E_TILES], I32)
        dst_idx = sb("dst_idx", [P, E_TILES], I32)
        dst_safe = sb("dst_safe", [P, E_TILES], I32)
        scatter_idx = sb("scatter_idx", [P, E_TILES], I32)
        edge_row = sb("edge_row", [P, E_TILES], I32)
        src_row = sb("src_row", [P, E_TILES], I32)
        dst_row_idx = sb("dst_row_idx", [P, E_TILES], I32)
        src_h = sb("src_h", [P, E_TILES, C])
        dst_h = sb("dst_h", [P, E_TILES, C])

        got_x_src, got_x_dst = sem("got_x_src"), sem("got_x_dst")
        map_scattered, got_src_row, got_dst_row = sem("map_scattered"), sem("got_src_row"), sem("got_dst_row")
        got_h = [sem(f"got_h{i}") for i in range(ROUNDS - 1)]
        x1_tile_got = [sem(f"x1_tile_got{k}") for k in range(RING)]
        got_x1_dst, dst_rebased = sem("got_x1_dst"), sem("dst_rebased")
        out_scattered = sem("out_scattered")
        ALL_TILES = 16 * E_TILES

        def gather(dest, table, idx, done, done_of=None):
            for t in range(E_TILES):
                yield lambda t=t: nc.gpsimd.indirect_dma_start(dest[:, t] if len(dest.shape) == 3 else dest[:, t:t + 1], None, table, bass.IndirectOffsetOnAxis(ap=idx[:, t:t + 1], axis=0)
                                             ).then_inc(done_of[t] if done_of else done, 16)

        with phase() as st:
            w_t_sb = sb("w_t_sb", [C, ROUNDS, C], stack=st)
            w_ih_sb = sb("w_ih_sb", [C, G3], stack=st)
            b_ih_at = sb("b_ih_at", [C + 1, G3], stack=st)
            dst_next = sb("dst_next", [P, E_TILES], I32, stack=st)
            runs_on = sb("runs_on", [P, E_TILES], stack=st)
            iota_map = sb("iota_map", [P, MAP_COLS], I32, stack=st)
            ones = sb("ones", [P, P], stack=st)
            pw = st.enter_context(nc.psum_tensor("pw", [C, ROUNDS, 512], F32))
            loaded, map_set = sem("loaded", st), sem("map_set", st)
            ones_set, ident_set, iota_set, rows_set = (sem(n, st) for n in ("ones_set", "ident_set", "iota_set", "rows_set"))
            fused, fused_out, idx_step = sem("fused", st), sem("fused_out", st), sem("idx_step", st)
            LOADS = 17 + ROUNDS
            block = st.enter_context(nc.Block())

            @block.sync
            def _(sp):
                for dest, source in (
                    (w_t_sb[:], w_t.rearrange("i k m -> k i m")), (w_ih_sb[:], w_ih_t), (w_h[0:C, :], w_hh_t),
                    (w_h[C:C + 1, :], b_hh), (b_ih_at[C:C + 1, :], b_ih),
                    (w_kv_sb[0:C, :], w_kv), (w_kv_sb[C:C + 1, :], b_kv), (w_q_sb[0:C, :], w_q), (w_q_sb[C:C + 1, :], b_q),
                    (w_e_sb[0:C, :], w_e), (w_e_sb[C:C + 1, :], b_e),
                    (src_idx[:], src_col), (dst_idx[:], dst_col), (dst_next[:], dst_next_col),
                ):
                    sp.dma_start(dest, source).then_inc(loaded, 16)
                for j in range(J):
                    sp.dma_start(b_in[:, j, :], b_ih[0:1, 2 * C:G3].partition_broadcast(P)).then_inc(loaded, 16)
                for i in range(ROUNDS):
                    sp.dma_start(w_f[i][C:C + 1, 2 * C:G3], b_ih[0:1, 2 * C:G3]).then_inc(loaded, 16)
                sp.wait_ge(iota_set, 1)
                sp.dma_start(row_of.rearrange("(p c) o -> p (c o)", p=P), iota_map[:]).then_inc(map_set, 16)
                sp.wait_ge(loaded, 16 * LOADS)
                sp.wait_ge(map_set, 16)

            @block.gpsimd
            def _(pool):
                nc.gpsimd.iota(iota_map[:], [[1, MAP_COLS]], base=0, channel_multiplier=MAP_COLS).then_inc(iota_set, 1)
                nc.gpsimd.iota(edge_row[:], [[1, E_TILES]], base=N_NODES, channel_multiplier=E_TILES).then_inc(rows_set, 1)
                nc.gpsimd.memset(ones[:], 1.0).then_inc(ones_set, 1)
                pool.wait_ge(ones_set, 1)
                nc.gpsimd.affine_select(out=ident[:], in_=ones[:], compare_op=ALU.is_equal, fill=0.0, base=0,
                                        pattern=[[-1, P]], channel_multiplier=1).then_inc(ident_set, 1)
                pool.wait_ge(ident_set, 1)
                pool.wait_ge(rows_set, 1)

            @block.tensor
            def _(pe):
                pe.wait_ge(loaded, 16 * LOADS)
                for i in range(ROUNDS):
                    last = nc.tensor.matmul(pw[:, i, 0:G3], w_t_sb[:, i, :], w_ih_sb[:], start=True, stop=True)
                last.then_inc(fused, 1)

            @block.vector
            def _(dve):
                dve.wait_ge(loaded, 16 * LOADS)
                nc.vector.tensor_tensor(w_h[C:C + 1, C:G3], w_h[C:C + 1, C:G3], b_ih_at[C:C + 1, 0:2 * C], ALU.add)
                for i in range(ROUNDS):
                    nc.vector.memset(w_f[i][C:C + 1, 0:2 * C], 0.0)
                nc.vector.tensor_scalar(dst_safe[:], dst_idx[:], float(N_NODES - 1), None, ALU.min)
                nc.vector.tensor_tensor(runs_on[:], dst_idx[:], dst_next[:], ALU.is_equal).then_inc(idx_step, 1)
                dve.wait_ge(idx_step, 1)
                nc.vector.scalar_tensor_tensor(out=scatter_idx[:], in0=runs_on[:], scalar=float(SKIP), in1=dst_idx[:],
                                               op0=ALU.mult, op1=ALU.add)
                dve.wait_ge(fused, 1)
                for i in range(ROUNDS):
                    last = nc.vector.tensor_copy(w_f[i][0:C, :], pw[:, i, 0:G3])
                last.then_inc(fused_out, 1)
                dve.wait_ge(fused_out, 1)

        def gru_phase(name, units, h_source, h_dests, norm=False, fused_w=None, x_source=None, pool_work=None, overlaps=False):
            edge = fused_w is not None
            with phase() as st:
                def ring(what, shape):
                    return [sb(f"{name}_{what}{k}", shape, stack=st) for k in range(RING)]

                def ring_sem(what):
                    return [sem(f"{name}_{what}{k}", st) for k in range(RING)]

                h_in = ring("h_in", [P, J, C])
                h = ring("h", [P, J, C]) if norm else h_in
                x_in = ring("x_in", [P, J, C]) if x_source is not None else None
                rz = ring("rz", [P, J, 2 * C])
                pre_n = ring("pre_n", [P, J, C])
                n = ring("n", [P, J, C])
                diff = ring("diff", [P, J, C])
                h_new = ring("h_new", [P, J, C])
                h_t = [sb(f"{name}_h_t{k}", [C + 1, U], stack=st) for k in range(2)]
                if norm:
                    stats, mean_var = ring("stats", [P, J, 6]), ring("mean_var", [P, J, 2])
                    rstd, shift = ring("rstd", [P, J]), ring("shift", [P, J])
                    minus_half = sb(f"{name}_minus_half", [P, J], stack=st)
                if edge:
                    v_in = ring("v_in", [P, J, C])
                    same = ring("same", [P, U])
                    goes_on = ring("goes_on", [P, U])
                    agg_t = [sb(f"{name}_agg_t{k}", [C + 1, U], stack=st) for k in range(2)]
                gates = [st.enter_context(nc.psum_tensor(f"{name}_gates{k}", [P, J, 512], F32)) for k in range(2)]
                turn = st.enter_context(nc.psum_tensor(f"{name}_turn", [P, 512], F32))
                agg_ps = st.enter_context(nc.psum_tensor(f"{name}_agg_ps", [P, 512], F32))

                in_loaded, stored = ring_sem("in_loaded"), ring_sem("stored")
                turned, h_t_ready, gates_done, rz_ready = (sem(f"{name}_{s}", st) for s in ("turned", "h_t_ready", "gates_done", "rz_ready"))
                mul_done, pre_ready, n_ready, diff_done, zdiff_done, blended, h_ready = (
                    sem(f"{name}_{s}", st) for s in ("mul_done", "pre_ready", "n_ready", "diff_done", "zdiff_done", "blended", "h_ready"))
                summed, carried, stats_seen, stats_made, moments, rstd_step, rstd_ready = (
                    sem(f"{name}_{s}", st) for s in ("summed", "carried", "stats_seen", "stats_made", "moments", "rstd_step", "rstd_ready"))
                ones_ready, n_and_x = sem(f"{name}_ones_ready", st), sem(f"{name}_n_and_x", st)
                IN = 16 * (1 + (x_source is not None) + 3 * edge)
                OUT = 16 * len(h_dests)
                block = st.enter_context(nc.Block())

                def load(sp, i, k):
                    if not exists(i, k, units):
                        return
                    done = in_loaded[k]
                    sp.dma_start(h_in[k][:], h_source(i, k)).then_inc(done, 16)
                    if x_source is not None:
                        sp.dma_start(x_in[k][:], x_source(i, k)).then_inc(done, 16)
                    if edge:
                        sp.dma_start(v_in[k][:], src_h[:, bass.ds((RING * i + k) * J, J), :]).then_inc(done, 16)
                        sp.dma_start(same[k][:], mask_rows(same_dram, i, k)).then_inc(done, 16)
                        sp.dma_start(goes_on[k][:], mask_rows(goes_on_dram, i, k)).then_inc(done, 16)

                @block.sync
                def _(sp):
                    for k in range(RING):
                        load(sp, 0, k)

                    def body(i, k):
                        u = RING * i + k
                        if norm:
                            sp.wait_ge(h_ready, u + 1)
                            load(sp, i + 1, k)
                        else:
                            sp.wait_ge(diff_done, u + 1)
                            if x_source is not None:
                                sp.wait_ge(n_and_x, u + 1)
                            load(sp, i + 1, k)
                        sp.wait_ge(blended, u + 1)
                        if overlaps and isinstance(u, int) and u == units - 1:
                            last = ahead(0, 0, u - 1)
                            sp.wait_ge(stored[last[1]], OUT * (last[0] + 1))
                        for dest in h_dests:
                            sp.dma_start(dest(i, k), h_new[k][:]).then_inc(stored[k], 16)

                    each_unit(sp, units, body)
                    for k in range(RING):
                        sp.wait_ge(stored[k], OUT * len(range(k, units, RING)))

                @block.gpsimd
                def _(pool):
                    todo = list(pool_work(pool)) if pool_work is not None else []
                    if norm:
                        nc.gpsimd.memset(minus_half[:], -0.5).then_inc(rstd_step, 1)
                        pool.wait_ge(rstd_step, 1)
                        for u in range(units):
                            k = u % RING
                            pool.wait_ge(moments, u + 1)
                            nc.gpsimd.tensor_scalar(rstd[k][:], mean_var[k][:, :, 1], EPS, None, ALU.add).then_inc(rstd_step, 1)
                            pool.wait_ge(rstd_step, 3 * u + 2)
                            nc.gpsimd.tensor_tensor(rstd[k][:], rstd[k][:], minus_half[:], ALU.pow).then_inc(rstd_step, 1)
                            pool.wait_ge(rstd_step, 3 * u + 3)
                            nc.gpsimd.tensor_tensor(shift[k][:], mean_var[k][:, :, 0], rstd[k][:], ALU.mult).then_inc(rstd_step, 1)
                            pool.wait_ge(rstd_step, 3 * u + 4)
                            nc.gpsimd.tensor_scalar(shift[k][:], shift[k][:], -1.0, None, ALU.mult).then_inc(rstd_ready, 1)
                            for task in todo[len(todo) * u // units:len(todo) * (u + 1) // units]:
                                task()
                    else:
                        for task in todo:
                            task()

                @block.tensor
                def _(pe):
                    def turn_unit(i, k):
                        u = RING * i + k
                        if norm:
                            pe.wait_ge(h_ready, u + 1)
                        else:
                            pe.wait_ge(in_loaded[k], IN * (i + 1))
                        for j in range(J):
                            last = nc.tensor.transpose(turn[0:C, P * j:P * (j + 1)], h[k][:, j, :], ident[:])
                        last.then_inc(turned, 1)
                        if edge:
                            for j in range(J):
                                last = nc.tensor.matmul(agg_ps[0:C, P * j:P * (j + 1)], v_in[k][:, j, :],
                                                        same[k][:, P * j:P * (j + 1)], start=True, stop=True)
                            last.then_inc(summed, 1)

                    turn_unit(0, 0)
                    pe.wait_ge(ones_ready, 1)

                    def body(i, k):
                        u, par = RING * i + k, k % 2
                        pe.wait_ge(h_t_ready, u + 1)
                        if edge:
                            pe.wait_ge(carried, u + 1)
                        nxt = ahead(i, k, 1)
                        if exists(*nxt, units):
                            turn_unit(*nxt)
                        wait(pe, pre_ready if edge else mul_done, u - 1)
                        for j in range(J):
                            last = nc.tensor.matmul(gates[par][:, j, 0:G3], h_t[par][:, P * j:P * (j + 1)], w_h[:],
                                                    start=True, stop=True)
                            if edge:
                                last = nc.tensor.matmul(gates[par][:, j, C:C + G3], agg_t[par][:, P * j:P * (j + 1)],
                                                        fused_w[:], start=False, stop=True, skip_group_check=True)
                        last.then_inc(gates_done, 1)

                    each_unit(pe, units, body)

                @block.scalar
                def _(act):
                    def turned_out(i, k):
                        u = RING * i + k
                        act.wait_ge(turned, u + 1)
                        nc.scalar.copy(h_t[k % 2][0:C, :], turn[0:C, 0:U]).then_inc(h_t_ready, 1)

                    def tanh(i, k):
                        u = RING * i + k
                        act.wait_ge(pre_ready, u + 1)
                        nc.scalar.activation(n[k][:], pre_n[k][:], ACTF.Tanh).then_inc(n_ready, 1)

                    def norm_out(i, k):
                        u = RING * i + k
                        act.wait_ge(rstd_ready, u + 1)
                        act.wait_ge(in_loaded[k], IN * (i + 1))
                        wait(act, blended, u - RING + 1)
                        for j in range(J):
                            last = nc.scalar.activation(h[k][:, j, :], h_in[k][:, j, :], ACTF.Relu,
                                                        bias=shift[k][:, j:j + 1], scale=rstd[k][:, j:j + 1])
                        last.then_inc(h_ready, 1)

                    if norm:
                        norm_out(0, 0)
                        norm_out(0, 1)
                    turned_out(0, 0)

                    def body(i, k):
                        u = RING * i + k
                        nxt = ahead(i, k, 1)
                        if exists(*nxt, units):
                            turned_out(*nxt)
                        act.wait_ge(gates_done, u + 1)
                        wait(act, blended, u - RING + 1)
                        nc.scalar.activation(rz[k][:], gates[k % 2][:, :, C:G3], ACTF.Sigmoid).then_inc(rz_ready, 1)
                        prev = ahead(i, k, -1)
                        if exists(*prev, units):
                            tanh(*prev)
                        nxt = ahead(i, k, 2)
                        if norm and exists(*nxt, units):
                            norm_out(*nxt)

                    each_unit(act, units, body)
                    tanh(*ahead(0, 0, units - 1))

                @block.vector
                def _(dve):
                    for par in range(2):
                        last = nc.vector.memset(h_t[par][C:C + 1, :], 1.0)
                        if edge:
                            nc.vector.memset(agg_t[par][C:C + 1, :], 1.0)
                            last = nc.vector.memset(agg_t[par][0:C, :], 0.0)
                    last.then_inc(ones_ready, 1)
                    dve.wait_ge(ones_ready, 1)

                    def moments_of(i, k):
                        u = RING * i + k
                        dve.wait_ge(in_loaded[k], IN * (i + 1))
                        wait(dve, rstd_ready, u - RING + 1)
                        for j in range(J):
                            last = nc.vector.bn_stats(stats[k][:, j, :], h_in[k][:, j, :])
                        last.then_inc(stats_made, 1)
                        dve.wait_ge(stats_made, u + 1)
                        dve.sem_inc(stats_seen, 1)
                        for j in range(J):
                            last = nc.vector.bn_aggr(mean_var[k][:, j, :], stats[k][:, j, :])
                        last.then_inc(moments, 1)

                    def carry(i, k):
                        u, par = RING * i + k, k % 2
                        dve.wait_ge(summed, u + 1)
                        for j in range(J):
                            before = agg_t[par][0:C, P * j - 1:P * j] if j else agg_t[1 - par][0:C, U - 1:U]
                            nc.vector.scalar_tensor_tensor(
                                out=agg_t[par][0:C, P * j:P * (j + 1)], in0=goes_on[k][0:C, P * j:P * (j + 1)], scalar=before,
                                in1=agg_ps[0:C, P * j:P * (j + 1)], op0=ALU.mult, op1=ALU.add).then_inc(
                                    carried if j == J - 1 else diff_carry, 1)
                            if j == J - 1:
                                dve.wait_ge(carried, u + 1)
                            else:
                                dve.wait_ge(diff_carry, (J - 1) * u + j + 1)

                    def blend_steps(i, k):
                        u = RING * i + k
                        dve.wait_ge(n_ready, u + 1)
                        nc.vector.tensor_tensor(diff[k][:], h[k][:], n[k][:], ALU.subtract).then_inc(diff_done, 1)
                        yield
                        dve.wait_ge(diff_done, u + 1)
                        nc.vector.tensor_tensor(diff[k][:], rz[k][:, :, C:2 * C], diff[k][:], ALU.mult).then_inc(zdiff_done, 1)
                        if x_source is not None:
                            nc.vector.tensor_tensor(n[k][:], x_in[k][:], n[k][:], ALU.add).then_inc(n_and_x, 1)
                        yield
                        dve.wait_ge(zdiff_done, u + 1)
                        if x_source is not None:
                            dve.wait_ge(n_and_x, u + 1)
                        wait(dve, stored[k], OUT * i)
                        nc.vector.tensor_tensor(h_new[k][:], n[k][:], diff[k][:], ALU.add).then_inc(blended, 1)

                    if norm:
                        for k in range(3):
                            moments_of(0, k)
                    if edge:
                        carry(0, 0)

                    def body(i, k):
                        u, par = RING * i + k, k % 2
                        nxt = ahead(i, k, 1)
                        if edge and exists(*nxt, units):
                            carry(*nxt)
                        prev = ahead(i, k, -1)
                        blend = blend_steps(*prev) if exists(*prev, units) else iter(())
                        dve.wait_ge(rz_ready, u + 1)
                        nc.vector.tensor_tensor(pre_n[k][:], gates[par][:, :, 0:C], rz[k][:, :, 0:C], ALU.mult).then_inc(mul_done, 1)
                        next(blend, None)
                        dve.wait_ge(mul_done, u + 1)
                        bias = gates[par][:, :, G3:G3 + C] if edge else b_in[:]
                        nc.vector.tensor_tensor(pre_n[k][:], bias, pre_n[k][:], ALU.add).then_inc(pre_ready, 1)
                        next(blend, None)
                        nxt = ahead(i, k, 3)
                        if norm and exists(*nxt, units):
                            moments_of(*nxt)
                        next(blend, None)

                    each_unit(dve, units, body)
                    for _ in blend_steps(*ahead(0, 0, units - 1)):
                        pass
                    dve.wait_ge(blended, units)

        diff_carry = None

        def pool_round1(pool):
            yield from gather(src_h, x, src_idx, got_x_src)
            yield from gather(dst_h, x, dst_safe, got_x_dst)
            for t in range(E_TILES):
                yield lambda t=t: nc.gpsimd.indirect_dma_start(row_of[:, :], bass.IndirectOffsetOnAxis(ap=scatter_idx[:, t:t + 1], axis=0),
                                             edge_row[:, t:t + 1], None, bounds_check=N_NODES - 1, oob_is_err=False
                                             ).then_inc(map_scattered, 16)
            yield lambda: pool.wait_ge(map_scattered, ALL_TILES)

        gru_phase("all1", DENSE_UNITS, dense_rows(x), [dense_rows(h_tab[0])], norm=True, pool_work=pool_round1, overlaps=True)

        with phase() as st:
            stats = [sb(f"prep_stats{n}", [P, E_TILES, 6], stack=st) for n in range(2)]
            moment = [sb(f"prep_moment{n}", [P, 5, E_TILES], stack=st) for n in range(2)]
            dst_all = [sb(f"dst_all{k}", [P, U + 1], I32, stack=st) for k in range(RING)]
            same_o = [sb(f"same_o{k}", [P, U], stack=st) for k in range(RING)]
            goes_o = [sb(f"goes_o{k}", [P, U], stack=st) for k in range(RING)]
            dst_loaded = [sem(f"dst_loaded{k}", st) for k in range(RING)]
            masks_stored = [sem(f"masks_stored{k}", st) for k in range(RING)]
            x_saved, masks_made, stats_made, moment_step, rooted, scaled, normed = (
                sem(s, st) for s in ("x_saved", "masks_made", "prep_stats_made", "moment_step", "rooted", "scaled", "prep_normed"))
            MEAN, DELTA, VAR, RSTD, SHIFT = range(5)
            block = st.enter_context(nc.Block())

            @block.sync
            def _(sp):
                def load(i, k):
                    if exists(i, k, EDGE_UNITS):
                        sp.dma_start(dst_all[k][:], dst_row[0:1, bass.ds((RING * i + k) * U, U + 1)].partition_broadcast(P)
                                     ).then_inc(dst_loaded[k], 16)

                for k in range(RING):
                    load(0, k)
                sp.wait_ge(got_x_dst, ALL_TILES)
                sp.dma_start(x_edge.rearrange("(p t) c -> p t c", p=P), dst_h[:]).then_inc(x_saved, 16)

                def body(i, k):
                    u = RING * i + k
                    sp.wait_ge(masks_made, 2 * (u + 1))
                    sp.dma_start(mask_rows(same_dram, i, k), same_o[k][:]).then_inc(masks_stored[k], 16)
                    sp.dma_start(mask_rows(goes_on_dram, i, k), goes_o[k][:]).then_inc(masks_stored[k], 16)
                    load(i + 1, k)

                each_unit(sp, EDGE_UNITS, body)
                for k in range(RING):
                    sp.wait_ge(masks_stored[k], 32 * len(range(k, EDGE_UNITS, RING)))

            @block.vector
            def _(dve):
                def stats_of(rows_h, n):
                    def body(i, k):
                        for j in range(J):
                            t = (RING * i + k) * J + j
                            last = nc.vector.bn_stats(stats[n][:, bass.ds(t, 1), :], rows_h[:, bass.ds(t, 1), :])
                        last.then_inc(stats_made, 1)

                    each_unit(dve, EDGE_UNITS, body)
                    dve.wait_ge(stats_made, EDGE_UNITS * (n + 1))
                    m, s = moment[n], stats[n]
                    done = 6 * n
                    nc.vector.tensor_tensor(m[:, MEAN], s[:, :, 1], s[:, :, 4], ALU.add).then_inc(moment_step, 1)
                    nc.vector.tensor_tensor(m[:, DELTA], s[:, :, 1], s[:, :, 4], ALU.subtract).then_inc(moment_step, 1)
                    nc.vector.tensor_tensor(m[:, VAR], s[:, :, 2], s[:, :, 5], ALU.add).then_inc(moment_step, 1)
                    dve.wait_ge(moment_step, done + 3)
                    nc.vector.tensor_tensor(m[:, DELTA], m[:, DELTA], m[:, DELTA], ALU.mult).then_inc(moment_step, 1)
                    nc.vector.tensor_scalar(m[:, VAR], m[:, VAR], 1.0 / C, EPS, ALU.mult, ALU.add).then_inc(moment_step, 1)
                    dve.wait_ge(moment_step, done + 5)
                    nc.vector.scalar_tensor_tensor(out=m[:, VAR], in0=m[:, DELTA], scalar=0.25, in1=m[:, VAR],
                                                   op0=ALU.mult, op1=ALU.add).then_inc(moment_step, 1)

                def scales_of(n):
                    m = moment[n]
                    dve.wait_ge(rooted, n + 1)
                    nc.vector.reciprocal(m[:, RSTD], m[:, DELTA]).then_inc(scaled, 1)
                    dve.wait_ge(scaled, 2 * n + 1)
                    nc.vector.scalar_tensor_tensor(out=m[:, SHIFT], in0=m[:, MEAN], scalar=-0.5, in1=m[:, RSTD],
                                                   op0=ALU.mult, op1=ALU.mult).then_inc(scaled, 1)

                dve.wait_ge(got_x_src, ALL_TILES)
                stats_of(src_h, 0)
                scales_of(0)
                dve.wait_ge(got_x_dst, ALL_TILES)
                stats_of(dst_h, 1)
                scales_of(1)

                def body(i, k):
                    u = RING * i + k
                    dve.wait_ge(dst_loaded[k], 16 * (i + 1))
                    wait(dve, masks_stored[k], 32 * i)
                    here = dst_all[k][:, 1:U + 1].rearrange("p (j e) -> p j e", j=J)
                    before = dst_all[k][:, 0:U].rearrange("p (j e) -> p j e", j=J)[:, :, 0:1]
                    mine = dst_idx[:, bass.ds(u * J, J)].unsqueeze(2)
                    nc.vector.tensor_tensor(same_o[k][:].rearrange("p (j e) -> p j e", j=J), here,
                                            mine.to_broadcast([P, J, P]), ALU.is_equal).then_inc(masks_made, 1)
                    nc.vector.tensor_tensor(goes_o[k][:].rearrange("p (j e) -> p j e", j=J), here,
                                            before.to_broadcast([P, J, P]), ALU.is_equal).then_inc(masks_made, 1)

                each_unit(dve, EDGE_UNITS, body)

            @block.scalar
            def _(act):
                for n, rows_h in enumerate((src_h, dst_h)):
                    m = moment[n]
                    act.wait_ge(moment_step, 6 * (n + 1))
                    nc.scalar.activation(m[:, DELTA], m[:, VAR], ACTF.Sqrt).then_inc(rooted, 1)
                    act.wait_ge(scaled, 2 * (n + 1))
                    if n:
                        act.wait_ge(x_saved, 16)

                    def body(i, k):
                        for j in range(J):
                            t = bass.ds((RING * i + k) * J + j, 1)
                            last = nc.scalar.activation(rows_h[:, t, :], rows_h[:, t, :], ACTF.Relu,
                                                        bias=m[:, SHIFT, t], scale=m[:, RSTD, t])
                        last.then_inc(normed, 1)

                    each_unit(act, EDGE_UNITS, body)
                act.wait_ge(normed, 2 * EDGE_UNITS)

            @block.gpsimd
            def _(pool):
                for task in gather(src_row, row_of[:, :], src_idx, got_src_row):
                    task()

        diff_carry = sem("tile_carried1")
        gru_phase("edge1", EDGE_UNITS, lambda i, k: dst_h[:, bass.ds((RING * i + k) * J, J), :], [edge_part(h_tab[0])], fused_w=w_f[0])

        def pool_round2(pool):
            yield lambda: pool.wait_ge(got_src_row, ALL_TILES)
            yield from gather(src_h, h_tab[0], src_row, got_h[0])
            yield lambda: pool.wait_ge(got_h[0], ALL_TILES)
            yield from gather(dst_row_idx, row_of[:, :], dst_safe, got_dst_row)
            yield lambda: pool.wait_ge(got_dst_row, ALL_TILES)

        gru_phase("all2", DENSE_UNITS, dense_rows(h_tab[0]), [dense_rows(h_tab[1])], pool_work=pool_round2, overlaps=True)
        diff_carry = sem("tile_carried2")
        gru_phase("edge2", EDGE_UNITS, edge_part(h_tab[0]), [edge_part(h_tab[1])], fused_w=w_f[1])

        def pool_round3(pool):
            yield from gather(src_h, h_tab[1], src_row, got_h[1])
            yield lambda: pool.wait_ge(got_h[1], ALL_TILES)

        FIRST_PART = DENSE_UNITS // 2 - 1
        assert (DENSE_UNITS - FIRST_PART) % RING and DENSE_UNITS % RING
        gru_phase("all3a", FIRST_PART, dense_rows(h_tab[1]), [dense_rows(out)], x_source=dense_rows(x), pool_work=pool_round3)
        diff_carry = sem("tile_carried3")
        gru_phase("edge3", EDGE_UNITS, edge_part(h_tab[1]), [edge_part(out), edge_rows(x1_edge)], fused_w=w_f[2], x_source=edge_rows(x_edge))

        def pool_x1_dst(pool):
            yield lambda: nc.gpsimd.tensor_scalar(dst_row_idx[:], dst_row_idx[:], float(-N_NODES), None, ALU.add).then_inc(dst_rebased, 1)
            yield lambda: pool.wait_ge(dst_rebased, 1)
            yield lambda: nc.gpsimd.tensor_scalar(dst_row_idx[:], dst_row_idx[:], 0.0, None, ALU.max).then_inc(dst_rebased, 1)
            yield lambda: pool.wait_ge(dst_rebased, 2)
            yield from gather(dst_h, x1_edge, dst_row_idx, got_x1_dst)
            yield lambda: pool.wait_ge(got_x1_dst, ALL_TILES)

        gru_phase("all3b", DENSE_UNITS - FIRST_PART, dense_rows(h_tab[1], FIRST_PART), [dense_rows(out, FIRST_PART)],
                  x_source=dense_rows(x, FIRST_PART), pool_work=pool_x1_dst, overlaps=True)

        with phase() as st:
            def two(what, shape):
                return [sb(f"att_{what}{k}", shape, stack=st) for k in range(2)]

            def ring(what, shape):
                return [sb(f"att_{what}{k}", shape, stack=st) for k in range(RING)]

            stats, mean_var, rstd, shift = (ring("stats", [P, 2, J, 6]), ring("mean_var", [P, 2 * J, 2]),
                                            ring("rstd", [P, 2 * J]), ring("shift", [P, 2 * J]))
            minus_half = sb("att_minus_half", [P, 2 * J], stack=st)
            same, goes_on, e_t = ring("same", [P, U]), ring("goes_on", [P, U]), ring("e_t", [C + 1, U])
            hs, hd = two("hs", [P, J, C]), two("hd", [P, J, C])
            hs_t, hd_t = two("hs_t", [C + 1, U]), two("hd_t", [C + 1, U])
            q, kq, score = two("q", [P, J, C]), two("kq", [P, J, C]), two("score", [P, J, HEADS])
            msg = two("msg", [P, J, M_COLS])
            sum_t = two("sum_t", [M_COLS, U])
            z_inv, mix = two("z_inv", [P, J, HEADS]), two("mix", [P, J, C])
            proj = st.enter_context(nc.psum_tensor("att_proj", [P, J, 512], F32))
            turn_s = st.enter_context(nc.psum_tensor("att_turn_s", [P, 512], F32))
            turn_d = st.enter_context(nc.psum_tensor("att_turn_d", [P, 512], F32))
            sums = st.enter_context(nc.psum_tensor("att_sums", [P, 512], F32))
            back = st.enter_context(nc.psum_tensor("att_back", [P, 512], F32))
            in_loaded = [sem(f"att_in_loaded{k}", st) for k in range(RING)]
            names = ("stats_seen", "stats_made", "moments", "rstd_step", "rstd_ready", "normed", "turned", "h_t_ready", "projected",
                     "q_ready", "kq_done", "kqe_done", "score_summed", "clipped", "weights_ready", "msg_ready", "summed", "carried",
                     "back_done", "z_added", "z_inverted", "mix_done", "mixed", "ones_ready")
            (stats_seen, stats_made, moments, rstd_step, rstd_ready, normed, turned, h_t_ready, projected, q_ready, kq_done, kqe_done,
             score_summed, clipped, weights_ready, msg_ready, summed, carried, back_done, z_added, z_inverted, mix_done, mixed,
             ones_ready) = (sem(f"att_{n}", st) for n in names)
            block = st.enter_context(nc.Block())

            @block.sync
            def _(sp):
                def load(i, k):
                    if exists(i, k, EDGE_UNITS):
                        u = RING * i + k
                        sp.dma_start(same[k][:], mask_rows(same_dram, i, k)).then_inc(in_loaded[k], 16)
                        sp.dma_start(goes_on[k][:], mask_rows(goes_on_dram, i, k)).then_inc(in_loaded[k], 16)
                        sp.dma_start(e_t[k][0:C, :], edge_t[:, bass.ds(u * U, U)]).then_inc(in_loaded[k], 16)

                for k in range(RING):
                    load(0, k)

                def body(i, k):
                    sp.wait_ge(carried, J * (RING * i + k + 1))
                    load(i + 1, k)

                each_unit(sp, EDGE_UNITS, body)

            @block.gpsimd
            def _(pool):
                nc.gpsimd.memset(minus_half[:], -0.5).then_inc(rstd_step, 1)
                pool.wait_ge(rstd_step, 1)
                tasks = list(gather(src_h, out, src_row, None, [x1_tile_got[t // J % RING] for t in range(E_TILES)]))
                AHEAD = RING * J
                for task in tasks[:AHEAD]:
                    task()
                for u in range(EDGE_UNITS):
                    k = u % RING
                    pool.wait_ge(moments, u + 1)
                    nc.gpsimd.tensor_scalar(rstd[k][:], mean_var[k][:, :, 1], EPS, None, ALU.add).then_inc(rstd_step, 1)
                    pool.wait_ge(rstd_step, 3 * u + 2)
                    nc.gpsimd.tensor_tensor(rstd[k][:], rstd[k][:], minus_half[:], ALU.pow).then_inc(rstd_step, 1)
                    pool.wait_ge(rstd_step, 3 * u + 3)
                    nc.gpsimd.tensor_tensor(shift[k][:], mean_var[k][:, :, 0], rstd[k][:], ALU.mult).then_inc(rstd_step, 1)
                    pool.wait_ge(rstd_step, 3 * u + 4)
                    nc.gpsimd.tensor_scalar(shift[k][:], shift[k][:], -1.0, None, ALU.mult).then_inc(rstd_ready, 1)
                    for task in tasks[AHEAD + J * u:AHEAD + J * (u + 1)]:
                        task()
                for k in range(RING):
                    pool.wait_ge(x1_tile_got[k], 16 * J * len(range(k, EDGE_UNITS, RING)))
                for t in range(E_TILES):
                    if t % J == 0:
                        pool.wait_ge(mixed, t // J + 1)
                    nc.gpsimd.indirect_dma_start(out, bass.IndirectOffsetOnAxis(ap=scatter_idx[:, t:t + 1], axis=0),
                                                 dst_h[:, t], None, bounds_check=N_NODES - 1, oob_is_err=False
                                                 ).then_inc(out_scattered, 16)
                pool.wait_ge(out_scattered, ALL_TILES)

            @block.tensor
            def _(pe):
                pe.wait_ge(ones_ready, 1)

                def turn_unit(i, k):
                    u = RING * i + k
                    pe.wait_ge(normed, u + 1)
                    wait(pe, h_t_ready, u)
                    for dest, source in ((turn_s, hs[k % 2]), (turn_d, hd[k % 2])):
                        for j in range(J):
                            last = nc.tensor.transpose(dest[0:C, P * j:P * (j + 1)], source[:, j, :], ident[:])
                    last.then_inc(turned, 1)

                def project(i, k):
                    u, par = RING * i + k, k % 2
                    pe.wait_ge(h_t_ready, u + 1)
                    pe.wait_ge(in_loaded[k], 48 * (i + 1))
                    wait(pe, msg_ready, u)
                    for j in range(J):
                        cols = slice(P * j, P * (j + 1))
                        nc.tensor.matmul(proj[:, j, 0:2 * C], hs_t[par][:, cols], w_kv_sb[:], start=True, stop=True)
                        nc.tensor.matmul(proj[:, j, 2 * C:3 * C], hd_t[par][:, cols], w_q_sb[:], start=True, stop=True)
                        last = nc.tensor.matmul(proj[:, j, 3 * C:4 * C], e_t[k][:, cols], w_e_sb[:], start=True, stop=True)
                    last.then_inc(projected, 1)

                def sum_edges(i, k):
                    u, par = RING * i + k, k % 2
                    pe.wait_ge(msg_ready, u + 1)
                    wait(pe, carried, J * u)
                    for j in range(J):
                        last = nc.tensor.matmul(sums[0:M_COLS, P * j:P * (j + 1)], msg[par][:, j, :], same[k][:, P * j:P * (j + 1)],
                                                start=True, stop=True)
                    last.then_inc(summed, 1)

                def turn_back(i, k):
                    u, par = RING * i + k, k % 2
                    pe.wait_ge(carried, J * (u + 1))
                    wait(pe, mix_done, u)
                    for j in range(J):
                        last = nc.tensor.transpose(back[:, M_COLS * j:M_COLS * (j + 1)], sum_t[par][:, P * j:P * (j + 1)],
                                                   ident[0:M_COLS, 0:M_COLS])
                    last.then_inc(back_done, 1)

                turn_unit(0, 0)

                def body(i, k):
                    project(i, k)
                    prev, nxt = ahead(i, k, -1), ahead(i, k, 1)
                    if exists(*prev, EDGE_UNITS):
                        sum_edges(*prev)
                    if exists(*nxt, EDGE_UNITS):
                        turn_unit(*nxt)
                    if exists(*prev, EDGE_UNITS):
                        turn_back(*prev)

                each_unit(pe, EDGE_UNITS, body)
                sum_edges(*ahead(0, 0, EDGE_UNITS - 1))
                turn_back(*ahead(0, 0, EDGE_UNITS - 1))

            @block.scalar
            def _(act):
                def norm_out(i, k):
                    u = RING * i + k
                    act.wait_ge(rstd_ready, u + 1)
                    wait(act, turned, u - 1)
                    for n, (rows_h, dest) in enumerate(((src_h, hs), (dst_h, hd))):
                        for j in range(J):
                            m = n * J + j
                            last = nc.scalar.activation(dest[k % 2][:, j, :].unsqueeze(1), rows_h[:, bass.ds(u * J + j, 1), :], ACTF.Relu,
                                                        bias=shift[k][:, m:m + 1], scale=rstd[k][:, m:m + 1])
                    last.then_inc(normed, 1)

                def turned_out(i, k):
                    u = RING * i + k
                    act.wait_ge(turned, u + 1)
                    wait(act, projected, u - 1)
                    nc.scalar.copy(hs_t[k % 2][0:C, :], turn_s[0:C, 0:U])
                    nc.scalar.copy(hd_t[k % 2][0:C, :], turn_d[0:C, 0:U]).then_inc(h_t_ready, 1)

                norm_out(0, 0)
                norm_out(0, 1)
                turned_out(0, 0)

                def body(i, k):
                    u = RING * i + k
                    act.wait_ge(projected, u + 1)
                    wait(act, kq_done, u - 1)
                    nc.scalar.activation(q[k % 2][:], proj[:, :, 2 * C:3 * C], ACTF.Copy, scale=float(HEAD_DIM) ** -0.5).then_inc(q_ready, 1)
                    nxt = ahead(i, k, 1)
                    if exists(*nxt, EDGE_UNITS):
                        turned_out(*nxt)
                    act.wait_ge(clipped, u + 1)
                    wait(act, summed, u - 1)
                    nc.scalar.activation(msg[k % 2][:, :, C:M_COLS], score[k % 2][:], ACTF.Exp).then_inc(weights_ready, 1)
                    nxt = ahead(i, k, 2)
                    if exists(*nxt, EDGE_UNITS):
                        norm_out(*nxt)

                each_unit(act, EDGE_UNITS, body)

            @block.vector
            def _(dve):
                for par in range(2):
                    nc.vector.memset(hs_t[par][C:C + 1, :], 1.0)
                    nc.vector.memset(hd_t[par][C:C + 1, :], 1.0)
                    nc.vector.memset(sum_t[par][:], 0.0)
                for k in range(RING):
                    last = nc.vector.memset(e_t[k][C:C + 1, :], 1.0)
                last.then_inc(ones_ready, 1)
                dve.wait_ge(ones_ready, 1)

                def stats_steps(i, k):
                    u = RING * i + k
                    dve.wait_ge(x1_tile_got[k], 16 * J * (i + 1))
                    wait(dve, rstd_ready, u - RING + 1)
                    for n, rows_h in enumerate((src_h, dst_h)):
                        for j in range(J):
                            last = nc.vector.bn_stats(stats[k][:, n, j, :].unsqueeze(1), rows_h[:, bass.ds(u * J + j, 1), :])
                    last.then_inc(stats_made, 1)
                    yield
                    dve.wait_ge(stats_made, u + 1)
                    dve.sem_inc(stats_seen, 1)
                    for n in range(2):
                        for j in range(J):
                            last = nc.vector.bn_aggr(mean_var[k][:, n * J + j, :], stats[k][:, n, j, :])
                    last.then_inc(moments, 1)

                def carry_steps(i, k):
                    u, par = RING * i + k, k % 2
                    dve.wait_ge(summed, u + 1)
                    for j in range(J):
                        before = sum_t[par][:, P * j - 1:P * j] if j else sum_t[1 - par][:, U - 1:U]
                        wait(dve, carried, J * u + j)
                        nc.vector.scalar_tensor_tensor(
                            out=sum_t[par][:, P * j:P * (j + 1)], in0=goes_on[k][0:M_COLS, P * j:P * (j + 1)], scalar=before,
                            in1=sums[0:M_COLS, P * j:P * (j + 1)], op0=ALU.mult, op1=ALU.add).then_inc(carried, 1)
                        yield

                def mix_steps(i, k):
                    u, par = RING * i + k, k % 2
                    dve.wait_ge(back_done, u + 1)
                    rows_b = back[:, 0:J * M_COLS].rearrange("p (j m) -> p j m", j=J)
                    nc.vector.tensor_scalar(z_inv[par][:], rows_b[:, :, C:M_COLS], 1e-6, None, ALU.add).then_inc(z_added, 1)
                    yield
                    dve.wait_ge(z_added, u + 1)
                    nc.vector.reciprocal(z_inv[par][:], z_inv[par][:]).then_inc(z_inverted, 1)
                    yield
                    dve.wait_ge(z_inverted, u + 1)
                    nc.vector.tensor_tensor(mix[par][:].rearrange("p j (h d) -> p j h d", h=HEADS),
                                            rows_b[:, :, 0:C].rearrange("p j (h d) -> p j h d", h=HEADS),
                                            z_inv[par][:].unsqueeze(3).to_broadcast([P, J, HEADS, HEAD_DIM]), ALU.mult).then_inc(mix_done, 1)
                    yield
                    dve.wait_ge(mix_done, u + 1)
                    mine = dst_h[:, bass.ds(u * J, J), :]
                    nc.vector.tensor_tensor(mine, mine, mix[par][:], ALU.add).then_inc(mixed, 1)

                for k in range(3):
                    for _ in stats_steps(0, k):
                        pass

                def body(i, k):
                    u, par = RING * i + k, k % 2
                    prev, later = ahead(i, k, -1), ahead(i, k, 3)
                    carry = carry_steps(*prev) if exists(*prev, EDGE_UNITS) else iter(())
                    mixing = mix_steps(*prev) if exists(*prev, EDGE_UNITS) else iter(())
                    taking = stats_steps(*later) if exists(*later, EDGE_UNITS) else iter(())
                    next(carry, None)
                    dve.wait_ge(q_ready, u + 1)
                    nc.vector.tensor_tensor(kq[par][:], proj[:, :, 0:C], q[par][:], ALU.mult).then_inc(kq_done, 1)
                    next(carry, None)
                    dve.wait_ge(kq_done, u + 1)
                    nc.vector.tensor_tensor(kq[par][:], proj[:, :, 3 * C:4 * C], kq[par][:], ALU.mult).then_inc(kqe_done, 1)
                    next(carry, None)
                    dve.wait_ge(kqe_done, u + 1)
                    wait(dve, weights_ready, u - 1)
                    nc.vector.reduce_sum(score[par][:], kq[par][:].rearrange("p j (h d) -> p j h d", h=HEADS), axis=AXX
                                         ).then_inc(score_summed, 1)
                    dve.wait_ge(score_summed, u + 1)
                    nc.vector.tensor_scalar(score[par][:], score[par][:], 5.0, -5.0, ALU.min, ALU.max).then_inc(clipped, 1)
                    next(taking, None)
                    dve.wait_ge(weights_ready, u + 1)
                    weights = msg[par][:, :, C:M_COLS].unsqueeze(3).to_broadcast([P, J, HEADS, HEAD_DIM])
                    nc.vector.tensor_tensor(msg[par][:, :, 0:C].rearrange("p j (h d) -> p j h d", h=HEADS),
                                            proj[:, :, C:2 * C].rearrange("p j (h d) -> p j h d", h=HEADS), weights,
                                            ALU.mult).then_inc(msg_ready, 1)
                    next(mixing, None)
                    next(taking, None)
                    next(mixing, None)
                    next(mixing, None)
                    next(mixing, None)

                each_unit(dve, EDGE_UNITS, body)
                for steps in (carry_steps, mix_steps):
                    for _ in steps(*ahead(0, 0, EDGE_UNITS - 1)):
                        pass
    return nc


def kernel(x, src, dst, edge_attr_96, L0_gnn_weight, L0_gnn_w_ih, L0_gnn_w_hh, L0_gnn_b_ih, L0_gnn_b_hh,
           L1_gnn_Wq, L1_gnn_bq, L1_gnn_Wk, L1_gnn_bk, L1_gnn_We, L1_gnn_be, L1_gnn_Wv, L1_gnn_bv):
    import numpy as _np
    import concourse.bacc as _bacc
    from concourse import mybir as _mybir
    from concourse.bass_utils import run_bass_kernel_spmd as _run

    a = _np.asarray
    src, dst, edge = a(src), a(dst), a(edge_attr_96)
    w_hh, b_hh, b_ih = a(L0_gnn_w_hh), a(L0_gnn_b_hh), a(L0_gnn_b_ih)
    pad = E_PAD - N_EDGES

    def columns(v):
        return _np.ascontiguousarray(v.reshape(E_TILES, P).T)

    def n_first(v):
        return _np.concatenate([v[2 * C:], v[:2 * C]], 0)

    src_p = _np.concatenate([src, _np.zeros(pad, src.dtype)])
    dst_p = _np.concatenate([dst, _np.full(pad + 1, NO_NODE, dst.dtype)])
    arrays = {
        "x": a(x),
        "src_col": columns(src_p),
        "dst_col": columns(dst_p[:-1]),
        "dst_next_col": columns(dst_p[1:]),
        "dst_row": _np.concatenate([_np.full(1, -1, dst.dtype), dst_p[:-1]])[None, :],
        "edge_t": _np.concatenate([edge, _np.zeros((pad, C), edge.dtype)], 0).T,
        "w_t": a(L0_gnn_weight).transpose(0, 2, 1),
        "w_ih_t": a(L0_gnn_w_ih).T,
        "w_hh_t": n_first(w_hh).T,
        "b_ih": b_ih[None, :],
        "b_hh": n_first(b_hh)[None, :],
        "w_kv": _np.concatenate([a(L1_gnn_Wk), a(L1_gnn_Wv)], 1),
        "b_kv": _np.concatenate([a(L1_gnn_bk), a(L1_gnn_bv)])[None, :],
        "w_q": a(L1_gnn_Wq), "b_q": a(L1_gnn_bq)[None, :],
        "w_e": a(L1_gnn_We), "b_e": a(L1_gnn_be)[None, :],
    }
    nc = _bacc.Bacc("TRN2", target_bir_lowering=False, num_devices=1)
    feed, args = {}, []
    for name, v in arrays.items():
        v = _np.ascontiguousarray(v)
        feed[f"in_{name}"] = v
        args.append(nc.dram_tensor(f"in_{name}", v.shape, _mybir.dt.from_np(v.dtype), kind="ExternalInput").ap())
    args.append(nc.dram_tensor("out", (N_NODES + E_PAD, C), F32, kind="ExternalOutput").ap())
    build(nc, *args)
    r = _run(nc, [feed], core_ids=[0])
    return r.results[0]["out"][:N_NODES]
```

```python
import numpy as np
import concourse.bass as bass
from concourse import mybir
from contextlib import ExitStack, contextmanager

N_NODES = 50000
N_EDGES = 12500
C = 96
ROUNDS = 3
HEADS = 8
HEAD_DIM = C // HEADS
P = 128
J = 3
U = P * J
G3 = 3 * C
DENSE_UNITS = -(-N_NODES // U)
LAST_DENSE_ROW = N_NODES - U
EDGE_UNITS = -(-N_EDGES // U)
E_TILES = EDGE_UNITS * J
E_PAD = E_TILES * P
MAP_COLS = -(-N_NODES // P)
M_COLS = C + HEADS
NO_NODE = N_NODES
SKIP = 1 << 16
EPS = 1e-5
RING = 8

F32 = mybir.dt.float32
I32 = mybir.dt.int32
ALU = mybir.AluOpType
ACTF = mybir.ActivationFunctionType
AXX = mybir.AxisListType.X


def wait(eng, sem, value):
    if isinstance(value, int) and value <= 0:
        return
    eng.wait_ge(sem, value)


def each_unit(eng, units, body):
    whole = units // RING
    for k in range(min(RING, units)):
        body(0, k)
    if whole > 2:
        with eng.Fori(1, whole - 1) as i:
            for k in range(RING):
                body(i, k)
    for u in range(max(RING, RING * (whole - 1)), units):
        body(u // RING, u % RING)


def ahead(i, k, d):
    return i + (k + d) // RING, (k + d) % RING


def width(i, k, units):
    return 1 if isinstance(i, int) and RING * i + k == units - 1 else 2


def exists(i, k, units):
    return not isinstance(i, int) or 0 <= RING * i + k < units


def build(nc, x, src_col, dst_col, dst_next_col, dst_row, edge_t, w_t, w_ih_t, w_hh_t, b_ih, b_hh,
          w_kv, b_kv, w_q, b_q, w_e, b_e, out):
    h_tab = [nc.dram_tensor(f"h{i}_table", (N_NODES + E_PAD, C), F32).ap() for i in (1, 2)] + [out]
    x1_edge = nc.dram_tensor("x1_edge", (E_PAD, C), F32).ap()
    x_edge = nc.dram_tensor("x_edge", (E_PAD, C), F32).ap()
    row_of = nc.dram_tensor("row_of", (P * MAP_COLS, 1), I32).ap()
    same_dram = nc.dram_tensor("same_dst", (EDGE_UNITS * P, U), F32).ap()
    goes_on_row = nc.dram_tensor("goes_on", (1, E_PAD), F32).ap()
    e_rows = nc.dram_tensor("e_rows", (EDGE_UNITS * P, J * C), F32).ap()

    def dense_rows(table, first=0):
        def rows(i, k, w):
            u = RING * i + k
            start = LAST_DENSE_ROW if isinstance(u, int) and first + u == DENSE_UNITS - 1 else (first + u) * U
            return table[bass.ds(start, w * U), :].rearrange("(w p j) c -> p w (j c)", p=P, j=J)
        return rows

    def edge_rows(array):
        return lambda i, k, w: array.rearrange("(p t) c -> p (t c)", p=P)[:, bass.ds((RING * i + k) * J * C, w * J * C)]

    def edge_part(table):
        return edge_rows(table[N_NODES:N_NODES + E_PAD, :])

    def mask_rows(rows, i, k):
        return rows[bass.ds((RING * i + k) * P, P), :]

    def mask_pair(rows, i, k, w):
        return rows[bass.ds((RING * i + k) * P, w * P), :].rearrange("(w p) e -> p w e", p=P)

    with ExitStack() as ctx:
        def sb(name, shape, dt=F32, stack=ctx):
            return stack.enter_context(nc.sbuf_tensor(name, shape, dt))

        def sem(name, stack=None):
            if stack is None:
                return ctx.enter_context(nc.semaphore(name))
            handle = nc.alloc_semaphore(name=name)
            taken.append(handle)
            return handle

        taken = []

        @contextmanager
        def phase():
            with ExitStack() as st:
                yield st
            nc.clear_and_free_semaphores(list(taken))
            taken.clear()
            nc.all_engine_barrier()

        ident = sb("ident", [P, P])
        w_h = sb("w_h", [C + 1, G3])
        w_f = [sb(f"w_f{i}", [C + 1, G3]) for i in range(ROUNDS)]
        w_kv_sb = sb("w_kv_sb", [C + 1, 2 * C])
        w_q_sb = sb("w_q_sb", [C + 1, C])
        w_e_sb = sb("w_e_sb", [C + 1, C])
        b_in = sb("b_in", [P, 2 * J, C])
        src_idx = sb("src_idx", [P, E_TILES], I32)
        dst_idx = sb("dst_idx", [P, E_TILES], I32)
        dst_safe = sb("dst_safe", [P, E_TILES], I32)
        scatter_idx = sb("scatter_idx", [P, E_TILES], I32)
        edge_row = sb("edge_row", [P, E_TILES], I32)
        src_row = sb("src_row", [P, E_TILES], I32)
        dst_row_idx = sb("dst_row_idx", [P, E_TILES], I32)
        src_h = sb("src_h", [P, E_TILES, C])
        dst_h = sb("dst_h", [P, E_TILES, C])

        got_x_src, got_x_dst = sem("got_x_src"), sem("got_x_dst")
        map_scattered, got_src_row, got_dst_row = sem("map_scattered"), sem("got_src_row"), sem("got_dst_row")
        got_h = [sem(f"got_h{i}") for i in range(ROUNDS - 1)]
        x1_tile_got = [sem(f"x1_tile_got{k}") for k in range(RING)]
        got_x1_dst, dst_rebased = sem("got_x1_dst"), sem("dst_rebased")
        out_scattered = sem("out_scattered")
        ALL_TILES = 16 * E_TILES

        def unit_of(buf, u):
            return buf[:, bass.ds(u * J, J)]

        def gather(dest, table, idx, done, done_of=None):
            for t in range(E_TILES):
                yield lambda t=t: nc.gpsimd.indirect_dma_start(dest[:, t] if len(dest.shape) == 3 else dest[:, t:t + 1], None, table, bass.IndirectOffsetOnAxis(ap=idx[:, t:t + 1], axis=0)
                                             ).then_inc(done_of[t] if done_of else done, 16)

        with phase() as st:
            w_t_sb = sb("w_t_sb", [C, ROUNDS, C], stack=st)
            w_ih_sb = sb("w_ih_sb", [C, G3], stack=st)
            b_ih_at = sb("b_ih_at", [C + 1, G3], stack=st)
            dst_next = sb("dst_next", [P, E_TILES], I32, stack=st)
            runs_on = sb("runs_on", [P, E_TILES], stack=st)
            iota_map = sb("iota_map", [P, MAP_COLS], I32, stack=st)
            ones = sb("ones", [P, P], stack=st)
            pw = st.enter_context(nc.psum_tensor("pw", [C, ROUNDS, 512], F32))
            loaded, map_set = sem("loaded", st), sem("map_set", st)
            ones_set, ident_set, iota_set, rows_set = (sem(n, st) for n in ("ones_set", "ident_set", "iota_set", "rows_set"))
            fused, fused_out, idx_step = sem("fused", st), sem("fused_out", st), sem("idx_step", st)
            LOADS = 14 + 2 * J + ROUNDS
            block = st.enter_context(nc.Block())

            @block.sync
            def _(sp):
                for dest, source in (
                    (w_t_sb[:], w_t.rearrange("i k m -> k i m")), (w_ih_sb[:], w_ih_t), (w_h[0:C, :], w_hh_t),
                    (w_h[C:C + 1, :], b_hh), (b_ih_at[C:C + 1, :], b_ih),
                    (w_kv_sb[0:C, :], w_kv), (w_kv_sb[C:C + 1, :], b_kv), (w_q_sb[0:C, :], w_q), (w_q_sb[C:C + 1, :], b_q),
                    (w_e_sb[0:C, :], w_e), (w_e_sb[C:C + 1, :], b_e),
                    (src_idx[:], src_col), (dst_idx[:], dst_col), (dst_next[:], dst_next_col),
                ):
                    sp.dma_start(dest, source).then_inc(loaded, 16)
                for j in range(2 * J):
                    sp.dma_start(b_in[:, j, :], b_ih[0:1, 2 * C:G3].partition_broadcast(P)).then_inc(loaded, 16)
                for i in range(ROUNDS):
                    sp.dma_start(w_f[i][C:C + 1, 2 * C:G3], b_ih[0:1, 2 * C:G3]).then_inc(loaded, 16)
                sp.wait_ge(iota_set, 1)
                sp.dma_start(row_of.rearrange("(p c) o -> p (c o)", p=P), iota_map[:]).then_inc(map_set, 16)
                sp.wait_ge(loaded, 16 * LOADS)
                sp.wait_ge(map_set, 16)

            @block.gpsimd
            def _(pool):
                nc.gpsimd.iota(iota_map[:], [[1, MAP_COLS]], base=0, channel_multiplier=MAP_COLS).then_inc(iota_set, 1)
                nc.gpsimd.iota(edge_row[:], [[1, E_TILES]], base=N_NODES, channel_multiplier=E_TILES).then_inc(rows_set, 1)
                nc.gpsimd.memset(ones[:], 1.0).then_inc(ones_set, 1)
                pool.wait_ge(ones_set, 1)
                nc.gpsimd.affine_select(out=ident[:], in_=ones[:], compare_op=ALU.is_equal, fill=0.0, base=0,
                                        pattern=[[-1, P]], channel_multiplier=1).then_inc(ident_set, 1)
                pool.wait_ge(ident_set, 1)
                pool.wait_ge(rows_set, 1)

            @block.tensor
            def _(pe):
                pe.wait_ge(loaded, 16 * LOADS)
                for i in range(ROUNDS):
                    last = nc.tensor.matmul(pw[:, i, 0:G3], w_t_sb[:, i, :], w_ih_sb[:], start=True, stop=True)
                last.then_inc(fused, 1)

            @block.vector
            def _(dve):
                dve.wait_ge(loaded, 16 * LOADS)
                nc.vector.tensor_tensor(w_h[C:C + 1, C:G3], w_h[C:C + 1, C:G3], b_ih_at[C:C + 1, 0:2 * C], ALU.add)
                for i in range(ROUNDS):
                    nc.vector.memset(w_f[i][C:C + 1, 0:2 * C], 0.0)
                nc.vector.tensor_scalar(dst_safe[:], dst_idx[:], float(N_NODES - 1), None, ALU.min)
                nc.vector.tensor_tensor(runs_on[:], dst_idx[:], dst_next[:], ALU.is_equal).then_inc(idx_step, 1)
                dve.wait_ge(idx_step, 1)
                nc.vector.scalar_tensor_tensor(out=scatter_idx[:], in0=runs_on[:], scalar=float(SKIP), in1=dst_idx[:],
                                               op0=ALU.mult, op1=ALU.add)
                dve.wait_ge(fused, 1)
                for i in range(ROUNDS):
                    last = nc.vector.tensor_copy(w_f[i][0:C, :], pw[:, i, 0:G3])
                last.then_inc(fused_out, 1)
                dve.wait_ge(fused_out, 1)

        def stats_to_moments(dve, s, m, step, done):
            nc.vector.tensor_tensor(m[:, MEAN], s[:, :, 1], s[:, :, 4], ALU.add).then_inc(step, 1)
            nc.vector.tensor_tensor(m[:, DELTA], s[:, :, 1], s[:, :, 4], ALU.subtract).then_inc(step, 1)
            nc.vector.tensor_tensor(m[:, VAR], s[:, :, 2], s[:, :, 5], ALU.add).then_inc(step, 1)
            dve.wait_ge(step, done + 3)
            nc.vector.tensor_tensor(m[:, DELTA], m[:, DELTA], m[:, DELTA], ALU.mult).then_inc(step, 1)
            nc.vector.tensor_scalar(m[:, VAR], m[:, VAR], 1.0 / C, EPS, ALU.mult, ALU.add).then_inc(step, 1)
            dve.wait_ge(step, done + 5)
            nc.vector.scalar_tensor_tensor(out=m[:, VAR], in0=m[:, DELTA], scalar=0.25, in1=m[:, VAR],
                                           op0=ALU.mult, op1=ALU.add).then_inc(step, 1)

        MEAN, DELTA, VAR, RSTD, SHIFT = range(5)
        MOMENT_STEPS = 6
        early = ExitStack()
        x_moment = sb("x_moment", [P, 5, DENSE_UNITS * J], stack=early)

        def pool_round1(pool):
            yield from gather(src_h, x, src_idx, got_x_src)
            yield from gather(dst_h, x, dst_safe, got_x_dst)
            for t in range(E_TILES):
                yield lambda t=t: nc.gpsimd.indirect_dma_start(row_of[:, :], bass.IndirectOffsetOnAxis(ap=scatter_idx[:, t:t + 1], axis=0),
                                             edge_row[:, t:t + 1], None, bounds_check=N_NODES - 1, oob_is_err=False
                                             ).then_inc(map_scattered, 16)
            yield lambda: pool.wait_ge(map_scattered, ALL_TILES)

        BESIDE_MOMENTS = 2 * E_TILES // 3

        with phase() as st:
            x_rows = sb("x_rows", [P, RING, U * C // P], stack=st)
            x_stats = sb("x_stats", [P, DENSE_UNITS * J, 6], stack=st)
            x_loaded = [sem(f"x_loaded{k}", st) for k in range(RING)]
            x_seen, x_step, x_rooted, x_scaled = (sem(n, st) for n in ("x_seen", "x_step", "x_rooted", "x_scaled"))
            block = st.enter_context(nc.Block())

            @block.sync
            def _(sp):
                def load(i, k):
                    if k % 2 == 0 and exists(i, k, DENSE_UNITS):
                        w = width(i, k, DENSE_UNITS)
                        sp.dma_start(x_rows[:, k:k + w], dense_rows(x)(i, k, w)).then_inc(x_loaded[k], 16)

                for k in range(RING):
                    load(0, k)

                def body(i, k):
                    if k % 2 == 0:
                        sp.wait_ge(x_seen, RING * i + k + width(i, k, DENSE_UNITS))
                        load(i + 1, k)

                each_unit(sp, DENSE_UNITS, body)

            @block.vector
            def _(dve):
                def body(i, k):
                    u = RING * i + k
                    dve.wait_ge(x_loaded[k - k % 2], 16 * (i + 1))
                    stats_u = unit_of(x_stats, u)
                    for j in range(J):
                        last = nc.vector.bn_stats(stats_u[:, j:j + 1], x_rows[:, k:k + 1, j * C:(j + 1) * C])
                    last.then_inc(x_seen, 1)

                each_unit(dve, DENSE_UNITS, body)
                dve.wait_ge(x_seen, DENSE_UNITS)
                stats_to_moments(dve, x_stats, x_moment, x_step, 0)
                dve.wait_ge(x_rooted, 1)
                nc.vector.reciprocal(x_moment[:, RSTD], x_moment[:, DELTA]).then_inc(x_scaled, 1)
                nc.vector.tensor_scalar(x_moment[:, MEAN], x_moment[:, MEAN], 0.5, None, ALU.mult).then_inc(x_scaled, 1)
                dve.wait_ge(x_scaled, 2)
                nc.vector.scalar_tensor_tensor(out=x_moment[:, SHIFT], in0=x_moment[:, MEAN], scalar=-1.0, in1=x_moment[:, RSTD],
                                               op0=ALU.mult, op1=ALU.mult).then_inc(x_scaled, 1)
                dve.wait_ge(x_scaled, 3)

            @block.scalar
            def _(act):
                act.wait_ge(x_step, MOMENT_STEPS)
                nc.scalar.activation(x_moment[:, DELTA], x_moment[:, VAR], ACTF.Sqrt).then_inc(x_rooted, 1)

            @block.gpsimd
            def _(pool):
                for task in list(pool_round1(pool))[:BESIDE_MOMENTS]:
                    task()

        def gru_phase(name, units, h_source, h_dests, moment=None, fused_w=None, x_source=None, pool_work=None, overlaps=False):
            edge, norm = fused_w is not None, moment is not None
            with phase() as st:
                def ring(what, cols=C):
                    return sb(f"{name}_{what}", [P, RING, J, cols], stack=st)

                def pair_sem(what):
                    return [sem(f"{name}_{what}{k}", st) for k in range(0, RING, 2)]

                h_in = ring("h_in")
                h = ring("x_normed") if norm else h_in
                x_in = ring("x_in") if x_source is not None else None
                rz, pre_n, n, diff, h_new = ring("rz", 2 * C), ring("pre_n"), ring("n"), ring("diff"), ring("h_new")
                h_t = [sb(f"{name}_h_t{k}", [C + 1, U], stack=st) for k in range(2)]
                if edge:
                    v_in = ring("v_in")
                    same = sb(f"{name}_same", [P, RING, U], stack=st)
                    goes_on = sb(f"{name}_goes_on", [C, RING, U], stack=st)
                    agg_t = [sb(f"{name}_agg_t{k}", [C + 1, U], stack=st) for k in range(2)]
                gates = [st.enter_context(nc.psum_tensor(f"{name}_gates{k}", [P, J, 512], F32)) for k in range(2)]
                turn = st.enter_context(nc.psum_tensor(f"{name}_turn", [P, 512], F32))
                agg_ps = st.enter_context(nc.psum_tensor(f"{name}_agg_ps", [P, 512], F32))

                in_loaded, x_loaded, stored = (pair_sem(s) for s in ("in_loaded", "x_loaded", "stored"))
                turned, h_t_ready, gates_done, rz_ready = (sem(f"{name}_{s}", st) for s in ("turned", "h_t_ready", "gates_done", "rz_ready"))
                mul_done, pre_ready, n_ready, diff_done, zdiff_done, blended = (
                    sem(f"{name}_{s}", st) for s in ("mul_done", "pre_ready", "n_ready", "diff_done", "zdiff_done", "blended"))
                summed, carried, carried_on, normed_act, normed_dve = (
                    sem(f"{name}_{s}", st) for s in ("summed", "carried", "carried_on", "normed_act", "normed_dve"))
                ones_ready, n_and_x = sem(f"{name}_ones_ready", st), sem(f"{name}_n_and_x", st)
                IN = 16 * (1 + 3 * edge)
                OUT = 16 * len(h_dests)
                NORM_AHEAD = 4
                STORE_LAG = 6 if norm else 2
                TANH_STEP = 0 if edge else 1
                block = st.enter_context(nc.Block())

                def flat(buf, k, w):
                    return buf[:, k:k + w].rearrange("p w j c -> p w (j c)")

                def flat_all(buf, k, w):
                    return buf[:, k:k + w].rearrange("p w j c -> p (w j c)") if edge else flat(buf, k, w)

                def dve_tiles(k):
                    return 1 + k % 2

                @block.sync
                def _(sp):
                    def load(i, k):
                        if not exists(i, k, units):
                            return
                        done, w = in_loaded[k // 2], width(i, k, units)
                        sp.dma_start(flat_all(h_in, k, w), h_source(i, k, w)).then_inc(done, 16)
                        if edge:
                            sp.dma_start(flat_all(v_in, k, w), src_h[:, bass.ds((RING * i + k) * J, w * J), :].rearrange("p t c -> p (t c)")
                                         ).then_inc(done, 16)
                            sp.dma_start(same[:, k:k + w], mask_pair(same_dram, i, k, w)).then_inc(done, 16)
                            sp.dma_start(goes_on[:, k:k + w].rearrange("p w e -> p (w e)"),
                                         goes_on_row[0:1, bass.ds((RING * i + k) * U, w * U)].partition_broadcast(C)).then_inc(done, 16)

                    def load_x(i, k):
                        if x_source is not None and exists(i, k, units):
                            w = width(i, k, units)
                            sp.dma_start(flat_all(x_in, k, w), x_source(i, k, w)).then_inc(x_loaded[k // 2], 16)

                    def store(i, k):
                        u, w = RING * i + k, width(i, k, units)
                        sp.wait_ge(blended, u + w)
                        if overlaps and isinstance(u, int) and u == units - 1:
                            last = ahead(0, 0, u - 2)
                            sp.wait_ge(stored[last[1] // 2], OUT * (last[0] + 1) + 1)
                        for dest in h_dests:
                            sp.dma_start(dest(i, k, w), flat_all(h_new, k, w)).then_inc(stored[k // 2], 16)

                    for k in range(0, RING, 2):
                        load(0, k)
                    for k in range(0, RING, 2):
                        load_x(0, k)

                    def body(i, k):
                        if k % 2:
                            return
                        prev = ahead(i, k, -STORE_LAG)
                        if exists(*prev, units):
                            refill = (prev[0] + 1, prev[1])
                            if x_source is not None and exists(*refill, units):
                                sp.wait_ge(n_and_x, RING * prev[0] + prev[1] + 2)
                                load_x(*refill)
                            store(*prev)
                        if exists(i + 1, k, units):
                            u = RING * i + k
                            if norm:
                                sp.wait_ge(normed_act, u + 2)
                                sp.wait_ge(normed_dve, u + 2)
                            else:
                                sp.wait_ge(diff_done, u + 2)
                                if edge:
                                    sp.wait_ge(carried, u + 2)
                            load(i + 1, k)

                    each_unit(sp, units, body)
                    end = units - 1 - (units - 1) % 2
                    for a in range(end + 2 - STORE_LAG, end + 2, 2):
                        store(*ahead(0, 0, a))
                    for k in range(0, RING, 2):
                        sp.wait_ge(stored[k // 2], OUT * len(range(k, units, RING)) + 1)

                @block.gpsimd
                def _(pool):
                    for task in pool_work(pool) if pool_work is not None else ():
                        task()

                @block.tensor
                def _(pe):
                    def turn_unit(i, k):
                        u = RING * i + k
                        if norm:
                            pe.wait_ge(normed_act, u + 1)
                            pe.wait_ge(normed_dve, u + 1)
                        else:
                            pe.wait_ge(in_loaded[k // 2], IN * (i + 1))
                        for j in range(J):
                            last = nc.tensor.transpose(turn[0:C, P * j:P * (j + 1)], h[:, k, j, :], ident[:])
                        last.then_inc(turned, 1)
                        if edge:
                            for j in range(J):
                                last = nc.tensor.matmul(agg_ps[0:C, P * j:P * (j + 1)], v_in[:, k, j, :],
                                                        same[:, k, P * j:P * (j + 1)], start=True, stop=True)
                            last.then_inc(summed, 1)

                    turn_unit(0, 0)
                    pe.wait_ge(ones_ready, 1)

                    def body(i, k):
                        u, par = RING * i + k, k % 2
                        pe.wait_ge(h_t_ready, u + 1)
                        if edge:
                            pe.wait_ge(carried, u + 1)
                        nxt = ahead(i, k, 1)
                        if exists(*nxt, units):
                            turn_unit(*nxt)
                        wait(pe, pre_ready if edge else mul_done, u - 1)
                        for j in range(J):
                            last = nc.tensor.matmul(gates[par][:, j, 0:G3], h_t[par][:, P * j:P * (j + 1)], w_h[:],
                                                    start=True, stop=True)
                            if edge:
                                last = nc.tensor.matmul(gates[par][:, j, C:C + G3], agg_t[par][:, P * j:P * (j + 1)],
                                                        fused_w[:], start=False, stop=True, skip_group_check=True)
                        last.then_inc(gates_done, 1)

                    each_unit(pe, units, body)

                @block.scalar
                def _(act):
                    def turned_out(i, k):
                        u = RING * i + k
                        act.wait_ge(turned, u + 1)
                        nc.scalar.activation(h_t[k % 2][0:C, :], turn[0:C, 0:U], ACTF.Relu if norm else ACTF.Copy).then_inc(h_t_ready, 1)

                    def tanh(i, k):
                        u, w = RING * i + k, width(i, k, units)
                        act.wait_ge(pre_ready, u + w)
                        nc.scalar.activation(n[:, k:k + w], pre_n[:, k:k + w], ACTF.Tanh).then_inc(n_ready, w)

                    def norm_out(i, k):
                        u = RING * i + k
                        act.wait_ge(in_loaded[k // 2], IN * (i + 1))
                        wait(act, diff_done, u - RING + 1)
                        shift, rstd = unit_of(moment[:, SHIFT], u), unit_of(moment[:, RSTD], u)
                        for j in range(dve_tiles(k), J):
                            last = nc.scalar.activation(h[:, k, j:j + 1, :], h_in[:, k, j:j + 1, :], ACTF.Identity,
                                                        bias=shift[:, j:j + 1], scale=rstd[:, j:j + 1])
                        last.then_inc(normed_act, 1)

                    if norm:
                        for k in range(NORM_AHEAD):
                            norm_out(0, k)
                    turned_out(0, 0)

                    def body(i, k):
                        u = RING * i + k
                        nxt = ahead(i, k, 1)
                        if exists(*nxt, units):
                            turned_out(*nxt)
                        act.wait_ge(gates_done, u + 1)
                        wait(act, zdiff_done, u - RING + 1)
                        nc.scalar.activation(rz[:, k], gates[k % 2][:, :, C:G3], ACTF.Sigmoid).then_inc(rz_ready, 1)
                        prev = ahead(i, k, -2 - TANH_STEP)
                        if k % 2 == TANH_STEP and exists(*prev, units):
                            tanh(*prev)
                        nxt = ahead(i, k, NORM_AHEAD)
                        if norm and exists(*nxt, units):
                            norm_out(*nxt)

                    each_unit(act, units, body)
                    end = ahead(0, 0, units - 1 - (units - 1) % 2)
                    if TANH_STEP and units % 2:
                        tanh(*ahead(*end, -2))
                    tanh(*end)

                @block.vector
                def _(dve):
                    for par in range(2):
                        last = nc.vector.memset(h_t[par][C:C + 1, :], 1.0)
                        if edge:
                            nc.vector.memset(agg_t[par][C:C + 1, :], 1.0)
                            last = nc.vector.memset(agg_t[par][0:C, :], 0.0)
                    last.then_inc(ones_ready, 1)
                    dve.wait_ge(ones_ready, 1)
                    for slots in stored:
                        dve.sem_inc(slots, 1)

                    def norm_dve(i, k):
                        u = RING * i + k
                        dve.wait_ge(in_loaded[k // 2], IN * (i + 1))
                        wait(dve, diff_done, u - RING + 1)
                        mean, rstd = unit_of(moment[:, MEAN], u), unit_of(moment[:, RSTD], u)
                        for j in range(dve_tiles(k)):
                            last = nc.vector.tensor_scalar(h[:, k, j:j + 1, :], h_in[:, k, j:j + 1, :], mean[:, j:j + 1], rstd[:, j:j + 1],
                                                           ALU.subtract, ALU.mult)
                        last.then_inc(normed_dve, 1)

                    def carry_steps(i, k):
                        u, par = RING * i + k, k % 2
                        for j in range(J):
                            if j == 0:
                                dve.wait_ge(summed, u + 1)
                            if j == 0:
                                wait(dve, carried, u)
                            else:
                                dve.wait_ge(carried_on, (J - 1) * u + j)
                            before = agg_t[par][0:C, P * j - 1:P * j] if j else agg_t[1 - par][0:C, U - 1:U]
                            nc.vector.scalar_tensor_tensor(
                                out=agg_t[par][0:C, P * j:P * (j + 1)], in0=goes_on[0:C, k, P * j:P * (j + 1)], scalar=before,
                                in1=agg_ps[0:C, P * j:P * (j + 1)], op0=ALU.mult, op1=ALU.add).then_inc(
                                    carried if j == J - 1 else carried_on, 1)
                            yield

                    def multiply(i, k):
                        u = RING * i + k
                        dve.wait_ge(rz_ready, u + 1)
                        wait(dve, n_ready, u - RING + 1)
                        nc.vector.tensor_tensor(pre_n[:, k], gates[k % 2][:, :, 0:C], rz[:, k, :, 0:C], ALU.mult).then_inc(mul_done, 1)

                    def add_edges(i, k):
                        u = RING * i + k
                        dve.wait_ge(mul_done, u + 1)
                        nc.vector.tensor_tensor(pre_n[:, k], gates[k % 2][:, :, G3:G3 + C], pre_n[:, k], ALU.add).then_inc(pre_ready, 1)

                    def add_bias(i, k):
                        u, w = RING * i + k, width(i, k, units)
                        dve.wait_ge(mul_done, u + w)
                        pre = pre_n[:, k:k + w].rearrange("p w j c -> p (w j) c")
                        nc.vector.tensor_tensor(pre, b_in[:, 0:w * J, :], pre, ALU.add).then_inc(pre_ready, w)

                    def take_diff(i, k):
                        u, w = RING * i + k, width(i, k, units)
                        dve.wait_ge(n_ready, u + w)
                        out_, h_, n_ = (b[:, k:k + w].rearrange("p w j c -> p (w j) c") for b in (diff, h, n))
                        if norm:
                            nc.vector.scalar_tensor_tensor(out=out_, in0=h_, scalar=0.0, in1=n_, op0=ALU.max, op1=ALU.subtract
                                                           ).then_inc(diff_done, w)
                        else:
                            nc.vector.tensor_tensor(out_, h_, n_, ALU.subtract).then_inc(diff_done, w)

                    def scale_diff(i, k):
                        u, w = RING * i + k, width(i, k, units)
                        dve.wait_ge(diff_done, u + w)
                        z = rz[:, k:k + w, :, C:2 * C]
                        nc.vector.tensor_tensor(diff[:, k:k + w], z, diff[:, k:k + w], ALU.mult).then_inc(zdiff_done, w)

                    def add_x(i, k):
                        w = width(i, k, units)
                        dve.wait_ge(x_loaded[k // 2], 16 * (i + 1))
                        nc.vector.tensor_tensor(n[:, k:k + w], x_in[:, k:k + w], n[:, k:k + w], ALU.add).then_inc(n_and_x, w)

                    def blend(i, k):
                        u, w = RING * i + k, width(i, k, units)
                        dve.wait_ge(zdiff_done, u + w)
                        if x_source is not None:
                            dve.wait_ge(n_and_x, u + w)
                        dve.wait_ge(stored[k // 2], OUT * i + 1)
                        nc.vector.tensor_tensor(h_new[:, k:k + w], n[:, k:k + w], diff[:, k:k + w], ALU.add).then_inc(blended, w)

                    if norm:
                        for k in range(NORM_AHEAD):
                            norm_dve(0, k)
                    if edge:
                        for _ in carry_steps(0, 0):
                            pass

                    def body(i, k):
                        nxt, later = ahead(i, k, 1), ahead(i, k, NORM_AHEAD)
                        last, older = ahead(i, k, -2 - k % 2), ahead(i, k, -4 - k % 2)
                        carry = carry_steps(*nxt) if edge and exists(*nxt, units) else iter(())
                        next(carry, None)
                        if edge:
                            if k % 2 == 0 and exists(*older, units):
                                scale_diff(*older)
                            if k % 2 and exists(*older, units):
                                blend(*older)
                            next(carry, None)
                            if k % 2 == 0 and x_source is not None and exists(*older, units):
                                add_x(*older)
                            if k % 2 and exists(*last, units):
                                take_diff(*last)
                            next(carry, None)
                            multiply(i, k)
                            add_edges(i, k)
                        else:
                            multiply(i, k)
                            if k % 2 == 0:
                                if exists(*last, units):
                                    add_bias(*last)
                                if exists(*older, units):
                                    scale_diff(*older)
                                    if x_source is not None:
                                        add_x(*older)
                            else:
                                if exists(*older, units):
                                    blend(*older)
                                if exists(*last, units):
                                    take_diff(*last)
                        if norm and exists(*later, units):
                            norm_dve(*later)

                    each_unit(dve, units, body)
                    end = ahead(0, 0, units - 1 - (units - 1) % 2)
                    older = ahead(*end, -2)
                    if not edge:
                        add_bias(*end)
                    if units % 2:
                        blend(*ahead(*end, -4))
                        take_diff(*older)
                    for pair in (older, end):
                        if pair == end:
                            take_diff(*pair)
                        scale_diff(*pair)
                        if x_source is not None:
                            add_x(*pair)
                        blend(*pair)
                    dve.wait_ge(blended, units)

        gru_phase("all1", DENSE_UNITS, dense_rows(x), [dense_rows(h_tab[0])], moment=x_moment,
                  pool_work=lambda pool: list(pool_round1(pool))[BESIDE_MOMENTS:], overlaps=True)
        early.close()

        with phase() as st:
            stats = [sb(f"prep_stats{n}", [P, E_TILES, 6], stack=st) for n in range(2)]
            moment = [sb(f"prep_moment{n}", [P, 5, E_TILES], stack=st) for n in range(2)]
            dst_all = [sb(f"dst_all{k}", [P, U + 1], I32, stack=st) for k in range(RING)]
            same_o = [sb(f"same_o{k}", [P, U], stack=st) for k in range(RING)]
            goes_o = sb("goes_o", [1, E_PAD], stack=st)
            e_t = [sb(f"prep_e_t{k}", [C + 1, U], stack=st) for k in range(RING)]
            e_out = [sb(f"prep_e_out{k}", [P, J * C], stack=st) for k in range(RING)]
            e_ps = [st.enter_context(nc.psum_tensor(f"prep_e_ps{k}", [P, 512], F32)) for k in range(2)]
            e_loaded = [sem(f"prep_e_loaded{k}", st) for k in range(RING)]
            e_stored = [sem(f"prep_e_stored{k}", st) for k in range(RING)]
            goes_on_saved = sem("goes_on_saved", st)
            e_ones, e_projected, e_copied, dve_scaled, dve_normed = (sem(s, st) for s in ("e_ones", "e_projected", "e_copied", "dve_scaled", "dve_normed"))
            SAVED = 3 * J
            ALL_SAVED = 16 * (E_TILES // SAVED)
            NORMS_A_ROUND = 6
            DVE_DST_UNITS = NORMS_A_ROUND * (EDGE_UNITS // RING - 1)
            dst_loaded = [sem(f"dst_loaded{k}", st) for k in range(RING)]
            masks_stored = [sem(f"masks_stored{k}", st) for k in range(RING)]
            x_saved, masks_made, stats_made, moment_step, rooted, scaled, normed = (
                sem(s, st) for s in ("x_saved", "masks_made", "prep_stats_made", "moment_step", "rooted", "scaled", "prep_normed"))
            block = st.enter_context(nc.Block())

            @block.sync
            def _(sp):
                def load(i, k):
                    if exists(i, k, EDGE_UNITS):
                        sp.dma_start(dst_all[k][:], dst_row[0:1, bass.ds((RING * i + k) * U, U + 1)].partition_broadcast(P)
                                     ).then_inc(dst_loaded[k], 16)

                for k in range(RING):
                    load(0, k)
                sp.wait_ge(got_x_dst, ALL_TILES)
                for a in range(0, E_TILES, SAVED):
                    sp.dma_start(x_edge.rearrange("(p t) c -> p t c", p=P)[:, a:a + SAVED], dst_h[:, a:a + SAVED]).then_inc(x_saved, 16)

                def body(i, k):
                    u = RING * i + k
                    sp.wait_ge(masks_made, 2 * (u + 1))
                    sp.dma_start(mask_rows(same_dram, i, k), same_o[k][:]).then_inc(masks_stored[k], 16)
                    load(i + 1, k)

                each_unit(sp, EDGE_UNITS, body)
                for k in range(RING):
                    sp.wait_ge(masks_stored[k], 16 * len(range(k, EDGE_UNITS, RING)))
                sp.dma_start(goes_on_row, goes_o[:]).then_inc(goes_on_saved, 16)
                sp.wait_ge(x_saved, ALL_SAVED)
                sp.wait_ge(goes_on_saved, 16)

            @block.gpsimd
            def _(pool):
                def load_edges(i, k):
                    if exists(i, k, EDGE_UNITS):
                        nc.gpsimd.dma_start(e_t[k][0:C, :], edge_t[:, bass.ds((RING * i + k) * U, U)]).then_inc(e_loaded[k], 16)

                for k in range(RING):
                    load_edges(0, k)

                def edge_body(i, k):
                    pool.wait_ge(e_copied, RING * i + k + 1)
                    nc.gpsimd.dma_start(mask_rows(e_rows, i, k), e_out[k][:]).then_inc(e_stored[k], 16)
                    load_edges(i + 1, k)

                each_unit(pool, EDGE_UNITS, edge_body)
                for k in range(RING):
                    pool.wait_ge(e_stored[k], 16 * len(range(k, EDGE_UNITS, RING)))

            @block.tensor
            def _(pe):
                pe.wait_ge(e_ones, 1)

                def body(i, k):
                    u = RING * i + k
                    pe.wait_ge(e_loaded[k], 16 * (i + 1))
                    wait(pe, e_copied, u - 1)
                    for j in range(J):
                        last = nc.tensor.matmul(e_ps[k % 2][:, C * j:C * (j + 1)], e_t[k][:, P * j:P * (j + 1)], w_e_sb[:], start=True, stop=True)
                    last.then_inc(e_projected, 1)

                each_unit(pe, EDGE_UNITS, body)

            @block.vector
            def _(dve):
                def stats_of(rows_h, n):
                    def body(i, k):
                        stats_u, rows_u = unit_of(stats[n], RING * i + k), unit_of(rows_h, RING * i + k)
                        for j in range(J):
                            last = nc.vector.bn_stats(stats_u[:, j:j + 1], rows_u[:, j:j + 1])
                        last.then_inc(stats_made, 1)

                    each_unit(dve, EDGE_UNITS, body)
                    dve.wait_ge(stats_made, EDGE_UNITS * (n + 1))
                    stats_to_moments(dve, stats[n], moment[n], moment_step, MOMENT_STEPS * n)

                def scales_of(n):
                    m = moment[n]
                    dve.wait_ge(rooted, n + 1)
                    nc.vector.reciprocal(m[:, RSTD], m[:, DELTA]).then_inc(scaled, 1)
                    dve.wait_ge(scaled, 2 * n + 1)
                    nc.vector.scalar_tensor_tensor(out=m[:, SHIFT], in0=m[:, MEAN], scalar=-0.5, in1=m[:, RSTD],
                                                   op0=ALU.mult, op1=ALU.mult).then_inc(scaled, 1)

                for k in range(RING):
                    last = nc.vector.memset(e_t[k][C:C + 1, :], 1.0)
                last.then_inc(e_ones, 1)
                dve.wait_ge(e_ones, 1)
                def body(i, k):
                    u = RING * i + k
                    dve.wait_ge(dst_loaded[k], 16 * (i + 1))
                    wait(dve, masks_stored[k], 16 * i)
                    here = dst_all[k][:, 1:U + 1].rearrange("p (j e) -> p j e", j=J)
                    before = dst_all[k][:, 0:U].rearrange("p (j e) -> p j e", j=J)[:, :, 0:1]
                    mine = dst_idx[:, bass.ds(u * J, J)].unsqueeze(2)
                    nc.vector.tensor_tensor(same_o[k][:].rearrange("p (j e) -> p j e", j=J), here,
                                            mine.to_broadcast([P, J, P]), ALU.is_equal).then_inc(masks_made, 1)
                    nc.vector.tensor_tensor(goes_o[:, bass.ds(u * U, U)].rearrange("p (j e) -> p j e", j=J), here[0:1],
                                            before[0:1].to_broadcast([1, J, P]), ALU.is_equal).then_inc(masks_made, 1)

                m = moment[1]

                def norm(u):
                    mine, rstd, shift = unit_of(dst_h, u), unit_of(m[:, RSTD], u), unit_of(m[:, SHIFT], u)
                    for j in range(J):
                        last = nc.vector.tensor_scalar(mine[:, j:j + 1], mine[:, j:j + 1], rstd[:, j:j + 1], shift[:, j:j + 1], ALU.mult, ALU.add)
                    last.then_inc(dve_scaled, 1)
                    dve.wait_ge(dve_scaled, u + 1)
                    nc.vector.tensor_scalar(mine, mine, 0.0, None, ALU.max).then_inc(dve_normed, 1)

                for k in range(RING):
                    body(0, k)
                dve.wait_ge(got_x_src, ALL_TILES)
                stats_of(src_h, 0)
                scales_of(0)
                dve.wait_ge(got_x_dst, ALL_TILES)
                stats_of(dst_h, 1)
                scales_of(1)
                dve.wait_ge(x_saved, ALL_SAVED)
                dve.wait_ge(scaled, 4)
                with dve.Fori(1, EDGE_UNITS // RING) as i:
                    for k in range(RING):
                        body(i, k)
                        if k < NORMS_A_ROUND:
                            norm(NORMS_A_ROUND * i + (k - NORMS_A_ROUND))
                for u in range(EDGE_UNITS - EDGE_UNITS % RING, EDGE_UNITS):
                    body(u // RING, u % RING)
                dve.wait_ge(dve_normed, DVE_DST_UNITS)

            @block.scalar
            def _(act):
                def norm(rows_h, m, u):
                    rows_u, rstd, shift = unit_of(rows_h, u), unit_of(m[:, RSTD], u), unit_of(m[:, SHIFT], u)
                    for j in range(J):
                        last = nc.scalar.activation(rows_u[:, j:j + 1], rows_u[:, j:j + 1], ACTF.Relu,
                                                    bias=shift[:, j:j + 1], scale=rstd[:, j:j + 1])
                    last.then_inc(normed, 1)

                def root(n):
                    m = moment[n]
                    act.wait_ge(moment_step, MOMENT_STEPS * (n + 1))
                    nc.scalar.activation(m[:, DELTA], m[:, VAR], ACTF.Sqrt).then_inc(rooted, 1)

                def edges_out(i, k):
                    u = RING * i + k
                    act.wait_ge(e_projected, u + 1)
                    wait(act, e_stored[k], 16 * i)
                    nc.scalar.copy(e_out[k][:], e_ps[k % 2][:, 0:J * C]).then_inc(e_copied, 1)

                EARLY = RING // 2
                for u in range(EARLY):
                    edges_out(u // RING, u % RING)
                root(0)
                act.wait_ge(scaled, 2)

                def source_body(i, k):
                    norm(src_h, moment[0], RING * i + k)
                    later = ahead(i, k, EARLY)
                    if exists(*later, EDGE_UNITS):
                        edges_out(*later)

                BEFORE_ROOT = 2 * RING
                for u in range(BEFORE_ROOT):
                    source_body(u // RING, u % RING)
                root(1)
                for u in range(BEFORE_ROOT, EDGE_UNITS):
                    source_body(u // RING, u % RING)
                act.wait_ge(scaled, 4)
                act.wait_ge(x_saved, ALL_SAVED)
                each_unit(act, EDGE_UNITS - DVE_DST_UNITS, lambda i, k: norm(dst_h, moment[1], RING * i + k + DVE_DST_UNITS))
                act.wait_ge(normed, 2 * EDGE_UNITS - DVE_DST_UNITS)

        gru_phase("edge1", EDGE_UNITS, lambda i, k, w: dst_h[:, bass.ds((RING * i + k) * J, w * J), :].rearrange("p t c -> p (t c)"), [edge_part(h_tab[0])], fused_w=w_f[0],
                  pool_work=lambda pool: gather(src_row, row_of[:, :], src_idx, got_src_row))

        def pool_round2(pool):
            yield lambda: pool.wait_ge(got_src_row, ALL_TILES)
            yield from gather(src_h, h_tab[0], src_row, got_h[0])
            yield lambda: pool.wait_ge(got_h[0], ALL_TILES)
            yield from gather(dst_row_idx, row_of[:, :], dst_safe, got_dst_row)
            yield lambda: pool.wait_ge(got_dst_row, ALL_TILES)

        gru_phase("all2", DENSE_UNITS, dense_rows(h_tab[0]), [dense_rows(h_tab[1])], pool_work=pool_round2, overlaps=True)
        gru_phase("edge2", EDGE_UNITS, edge_part(h_tab[0]), [edge_part(h_tab[1])], fused_w=w_f[1])

        def pool_round3(pool):
            yield from gather(src_h, h_tab[1], src_row, got_h[1])
            yield lambda: pool.wait_ge(got_h[1], ALL_TILES)

        FIRST_PART = DENSE_UNITS // 2 - 1
        assert (DENSE_UNITS - FIRST_PART) % RING and DENSE_UNITS % RING
        gru_phase("all3a", FIRST_PART, dense_rows(h_tab[1]), [dense_rows(out)], x_source=dense_rows(x), pool_work=pool_round3)
        gru_phase("edge3", EDGE_UNITS, edge_part(h_tab[1]), [edge_part(out), edge_rows(x1_edge)], fused_w=w_f[2], x_source=edge_rows(x_edge))

        def pool_x1_dst(pool):
            yield lambda: nc.gpsimd.tensor_scalar(dst_row_idx[:], dst_row_idx[:], float(-N_NODES), None, ALU.add).then_inc(dst_rebased, 1)
            yield lambda: pool.wait_ge(dst_rebased, 1)
            yield lambda: nc.gpsimd.tensor_scalar(dst_row_idx[:], dst_row_idx[:], 0.0, None, ALU.max).then_inc(dst_rebased, 1)
            yield lambda: pool.wait_ge(dst_rebased, 2)
            yield from gather(dst_h, x1_edge, dst_row_idx, got_x1_dst)
            yield lambda: pool.wait_ge(got_x1_dst, ALL_TILES)

        gru_phase("all3b", DENSE_UNITS - FIRST_PART, dense_rows(h_tab[1], FIRST_PART), [dense_rows(out, FIRST_PART)],
                  x_source=dense_rows(x, FIRST_PART), pool_work=pool_x1_dst, overlaps=True)

        with phase() as st:
            def two(what, shape):
                return [sb(f"att_{what}{k}", shape, stack=st) for k in range(2)]

            def ring(what, shape):
                return [sb(f"att_{what}{k}", shape, stack=st) for k in range(RING)]

            NORM_RING = 4
            NORM_AHEAD = NORM_RING - 1
            src_stats, src_moment = sb("att_src_stats", [P, RING * J, 6], stack=st), sb("att_src_moment", [P, 5, RING * J], stack=st)
            dst_stats, dst_moment = sb("att_dst_stats", [P, E_TILES, 6], stack=st), sb("att_dst_moment", [P, 5, E_TILES], stack=st)
            same, goes_on, e = ring("same", [P, U]), ring("goes_on", [M_COLS, U]), ring("e", [P, J * C])
            hs, hd = ([sb(f"att_{n}{k}", [P, J, C], stack=st) for k in range(NORM_RING)] for n in ("hs", "hd"))
            hs_t, hd_t = two("hs_t", [C + 1, U]), two("hd_t", [C + 1, U])
            q, kq, score = two("q", [P, J, C]), two("kq", [P, J, C]), two("score", [P, J, HEADS])
            msg = two("msg", [P, J, M_COLS])
            sum_t = two("sum_t", [M_COLS, U])
            z_inv, mix = two("z_inv", [P, J, HEADS]), two("mix", [P, J, C])
            projs = [st.enter_context(nc.psum_tensor(f"att_proj{k}", [P, J, 512], F32)) for k in range(2)]
            turn = st.enter_context(nc.psum_tensor("att_turn", [P, 512], F32))
            sums = st.enter_context(nc.psum_tensor("att_sums", [P, 512], F32))
            in_loaded = [sem(f"att_in_loaded{k}", st) for k in range(RING)]
            names = ("dst_seen", "src_seen", "moment_step", "rooted", "scaled", "s_normed", "d_normed", "s_turned", "d_turned", "s_t_ready", "h_t_ready", "projected",
                     "q_ready", "kq_done", "kqe_done", "score_summed", "clipped", "weights_ready", "msg_ready", "summed", "carried",
                     "back_done", "z_added", "z_inverted", "mix_done", "mixed", "ones_ready")
            (dst_seen, src_seen, moment_step, rooted, scaled, s_normed, d_normed, s_turned, d_turned, s_t_ready, h_t_ready, projected, q_ready, kq_done, kqe_done,
             score_summed, clipped, weights_ready, msg_ready, summed, carried, back_done, z_added, z_inverted, mix_done, mixed,
             ones_ready) = (sem(f"att_{n}", st) for n in names)
            block = st.enter_context(nc.Block())

            @block.sync
            def _(sp):
                def load(i, k):
                    if exists(i, k, EDGE_UNITS):
                        sp.dma_start(same[k][:], mask_rows(same_dram, i, k)).then_inc(in_loaded[k], 16)
                        sp.dma_start(goes_on[k][:], goes_on_row[0:1, bass.ds((RING * i + k) * U, U)].partition_broadcast(M_COLS)
                                     ).then_inc(in_loaded[k], 16)
                        sp.dma_start(e[k][:], mask_rows(e_rows, i, k)).then_inc(in_loaded[k], 16)

                for k in range(RING):
                    load(0, k)

                def body(i, k):
                    sp.wait_ge(carried, J * (RING * i + k + 1))
                    load(i + 1, k)

                each_unit(sp, EDGE_UNITS, body)

            @block.gpsimd
            def _(pool):
                for t, task in enumerate(gather(src_h, out, src_row, None, [x1_tile_got[t // J % RING] for t in range(E_TILES)])):
                    u = t // J
                    if t % J == 0 and u >= RING:
                        pool.wait_ge(x1_tile_got[u % RING], 16 * J * (u // RING))
                    task()
                for k in range(RING):
                    pool.wait_ge(x1_tile_got[k], 16 * J * len(range(k, EDGE_UNITS, RING)))
                for t in range(E_TILES):
                    if t % J == 0:
                        pool.wait_ge(mixed, t // J + 1)
                    nc.gpsimd.indirect_dma_start(out, bass.IndirectOffsetOnAxis(ap=scatter_idx[:, t:t + 1], axis=0),
                                                 dst_h[:, t], None, bounds_check=N_NODES - 1, oob_is_err=False
                                                 ).then_inc(out_scattered, 16)
                pool.wait_ge(out_scattered, ALL_TILES)

            @block.tensor
            def _(pe):
                pe.wait_ge(ones_ready, 1)

                def turn_sources(i, k):
                    u = RING * i + k
                    pe.wait_ge(s_normed, u + 1)
                    wait(pe, h_t_ready, u)
                    for j in range(J):
                        last = nc.tensor.transpose(turn[0:C, P * j:P * (j + 1)], hs[k % NORM_RING][:, j, :], ident[:])
                    last.then_inc(s_turned, 1)

                def turn_destinations(i, k):
                    u = RING * i + k
                    pe.wait_ge(d_normed, u + 1)
                    pe.wait_ge(s_t_ready, u + 1)
                    for j in range(J):
                        last = nc.tensor.transpose(turn[0:C, P * j:P * (j + 1)], hd[k % NORM_RING][:, j, :], ident[:])
                    last.then_inc(d_turned, 1)

                def project(i, k, tiles=range(J)):
                    u, par = RING * i + k, k % 2
                    pe.wait_ge(h_t_ready, u + 1)
                    wait(pe, msg_ready, u - 1)
                    proj = projs[par]
                    for j in tiles:
                        cols = slice(P * j, P * (j + 1))
                        nc.tensor.matmul(proj[:, j, 0:2 * C], hs_t[par][:, cols], w_kv_sb[:], start=True, stop=True)
                        last = nc.tensor.matmul(proj[:, j, 2 * C:3 * C], hd_t[par][:, cols], w_q_sb[:], start=True, stop=True)
                    if j == J - 1:
                        last.then_inc(projected, 1)

                def sum_edges(i, k):
                    u, par = RING * i + k, k % 2
                    pe.wait_ge(in_loaded[k], 48 * (i + 1))
                    pe.wait_ge(msg_ready, u + 1)
                    wait(pe, mix_done, u)
                    for j in range(J):
                        last = nc.tensor.matmul(sums[0:M_COLS, P * j:P * (j + 1)], msg[par][:, j, :], same[k][:, P * j:P * (j + 1)],
                                                start=True, stop=True)
                    last.then_inc(summed, 1)

                def turn_back(i, k):
                    u, par = RING * i + k, k % 2
                    pe.wait_ge(carried, J * (u + 1))
                    for j in range(J):
                        last = nc.tensor.transpose(sums[:, M_COLS * j:M_COLS * (j + 1)], sum_t[par][:, P * j:P * (j + 1)],
                                                   ident[0:M_COLS, 0:M_COLS])
                    last.then_inc(back_done, 1)

                for k in range(2):
                    turn_sources(0, k)
                    turn_destinations(0, k)
                project(0, 0)

                def body(i, k):
                    prev, nxt, later = ahead(i, k, -1), ahead(i, k, 1), ahead(i, k, 2)
                    if exists(*prev, EDGE_UNITS):
                        sum_edges(*prev)
                    if exists(*nxt, EDGE_UNITS):
                        project(*nxt, range(J - 1))
                    if exists(*prev, EDGE_UNITS):
                        turn_back(*prev)
                    if exists(*nxt, EDGE_UNITS):
                        project(*nxt, range(J - 1, J))
                    if exists(*later, EDGE_UNITS):
                        turn_sources(*later)
                    if exists(*later, EDGE_UNITS):
                        turn_destinations(*later)

                each_unit(pe, EDGE_UNITS, body)
                sum_edges(*ahead(0, 0, EDGE_UNITS - 1))
                turn_back(*ahead(0, 0, EDGE_UNITS - 1))

            @block.scalar
            def _(act):
                def norm_sources(i, k):
                    u = RING * i + k
                    if k == 0:
                        act.wait_ge(scaled, 2 * (i + 2))
                    wait(act, d_turned, u - NORM_RING + 1)
                    rows_u = unit_of(src_h, u)
                    for j in range(J):
                        m = k * J + j
                        last = nc.scalar.activation(hs[k % NORM_RING][:, j:j + 1, :], rows_u[:, j:j + 1], ACTF.Relu,
                                                    bias=src_moment[:, SHIFT, m:m + 1], scale=src_moment[:, RSTD, m:m + 1])
                    last.then_inc(s_normed, 1)

                def norm_destinations(i, k):
                    u = RING * i + k
                    rows_u, shift, rstd = unit_of(dst_h, u), unit_of(dst_moment[:, SHIFT], u), unit_of(dst_moment[:, RSTD], u)
                    for j in range(J):
                        last = nc.scalar.activation(hd[k % NORM_RING][:, j:j + 1, :], rows_u[:, j:j + 1], ACTF.Relu,
                                                    bias=shift[:, j:j + 1], scale=rstd[:, j:j + 1])
                    last.then_inc(d_normed, 1)

                def root(m, after):
                    act.wait_ge(moment_step, after)
                    nc.scalar.activation(m[:, DELTA], m[:, VAR], ACTF.Sqrt).then_inc(rooted, 1)

                def sources_out(i, k):
                    u = RING * i + k
                    wait(act, projected, u - 1)
                    act.wait_ge(s_turned, u + 1)
                    nc.scalar.copy(hs_t[k % 2][0:C, :], turn[0:C, 0:U]).then_inc(s_t_ready, 1)

                def destinations_out(i, k):
                    u = RING * i + k
                    act.wait_ge(d_turned, u + 1)
                    nc.scalar.copy(hd_t[k % 2][0:C, :], turn[0:C, 0:U]).then_inc(h_t_ready, 1)

                root(dst_moment, MOMENT_STEPS)
                act.wait_ge(scaled, 2)
                for k in range(NORM_AHEAD):
                    norm_destinations(0, k)
                root(src_moment, 2 * MOMENT_STEPS)
                for k in range(NORM_AHEAD):
                    norm_sources(0, k)
                for k in range(2):
                    sources_out(0, k)
                    destinations_out(0, k)

                def query(i, k):
                    u = RING * i + k
                    act.wait_ge(projected, u + 1)
                    wait(act, kq_done, u - 1)
                    nc.scalar.activation(q[k % 2][:], projs[k % 2][:, :, 2 * C:3 * C], ACTF.Copy, scale=float(HEAD_DIM) ** -0.5).then_inc(q_ready, 1)

                query(0, 0)

                def body(i, k):
                    u = RING * i + k
                    nxt, later, normed = ahead(i, k, 1), ahead(i, k, 2), ahead(i, k, NORM_AHEAD)
                    if exists(*normed, EDGE_UNITS):
                        norm_sources(*normed)
                    act.wait_ge(clipped, u + 1)
                    wait(act, summed, u - 1)
                    nc.scalar.activation(msg[k % 2][:, :, C:M_COLS], score[k % 2][:], ACTF.Exp).then_inc(weights_ready, 1)
                    if exists(*nxt, EDGE_UNITS):
                        query(*nxt)
                    if exists(*later, EDGE_UNITS):
                        sources_out(*later)
                    if exists(*normed, EDGE_UNITS):
                        norm_destinations(*normed)
                    if exists(*later, EDGE_UNITS):
                        destinations_out(*later)
                    if k == RING // 2 and exists(i + 1, 0, EDGE_UNITS):
                        root(src_moment, MOMENT_STEPS * (i + 3))

                each_unit(act, EDGE_UNITS, body)

            @block.vector
            def _(dve):
                for par in range(2):
                    nc.vector.memset(hs_t[par][C:C + 1, :], 1.0)
                    nc.vector.memset(hd_t[par][C:C + 1, :], 1.0)
                    last = nc.vector.memset(sum_t[par][:], 0.0)
                last.then_inc(ones_ready, 1)
                dve.wait_ge(ones_ready, 1)

                def source_stats(i, k):
                    u = RING * i + k
                    dve.wait_ge(x1_tile_got[k], 16 * J * (i + 1))
                    rows_u = unit_of(src_h, u)
                    for j in range(J):
                        m = k * J + j
                        last = nc.vector.bn_stats(src_stats[:, m:m + 1, :], rows_u[:, j:j + 1])
                    last.then_inc(src_seen, 1)

                def scales(m, r):
                    dve.wait_ge(rooted, r + 1)
                    nc.vector.reciprocal(m[:, RSTD], m[:, DELTA]).then_inc(scaled, 1)
                    dve.wait_ge(scaled, 2 * r + 1)
                    nc.vector.scalar_tensor_tensor(out=m[:, SHIFT], in0=m[:, MEAN], scalar=-0.5, in1=m[:, RSTD],
                                                   op0=ALU.mult, op1=ALU.mult).then_inc(scaled, 1)

                def carry_steps(i, k):
                    u, par = RING * i + k, k % 2
                    dve.wait_ge(summed, u + 1)
                    for j in range(J):
                        before = sum_t[par][:, P * j - 1:P * j] if j else sum_t[1 - par][:, U - 1:U]
                        wait(dve, carried, J * u + j)
                        nc.vector.scalar_tensor_tensor(
                            out=sum_t[par][:, P * j:P * (j + 1)], in0=goes_on[k][0:M_COLS, P * j:P * (j + 1)], scalar=before,
                            in1=sums[0:M_COLS, P * j:P * (j + 1)], op0=ALU.mult, op1=ALU.add).then_inc(carried, 1)
                        yield

                def mix_steps(i, k):
                    u, par = RING * i + k, k % 2
                    dve.wait_ge(back_done, u + 1)
                    rows_b = sums[:, 0:J * M_COLS].rearrange("p (j m) -> p j m", j=J)
                    nc.vector.tensor_scalar(z_inv[par][:], rows_b[:, :, C:M_COLS], 1e-6, None, ALU.add).then_inc(z_added, 1)
                    yield
                    dve.wait_ge(z_added, u + 1)
                    nc.vector.reciprocal(z_inv[par][:], z_inv[par][:]).then_inc(z_inverted, 1)
                    yield
                    dve.wait_ge(z_inverted, u + 1)
                    nc.vector.tensor_tensor(mix[par][:].rearrange("p j (h d) -> p j h d", h=HEADS),
                                            rows_b[:, :, 0:C].rearrange("p j (h d) -> p j h d", h=HEADS),
                                            z_inv[par][:].unsqueeze(3).to_broadcast([P, J, HEADS, HEAD_DIM]), ALU.mult).then_inc(mix_done, 1)
                    yield
                    dve.wait_ge(mix_done, u + 1)
                    mine = dst_h[:, bass.ds(u * J, J), :]
                    nc.vector.tensor_tensor(mine, mine, mix[par][:], ALU.add).then_inc(mixed, 1)

                def destination_stats(i, k):
                    stats_u, rows_u = unit_of(dst_stats, RING * i + k), unit_of(dst_h, RING * i + k)
                    for j in range(J):
                        last = nc.vector.bn_stats(stats_u[:, j:j + 1], rows_u[:, j:j + 1])
                    last.then_inc(dst_seen, 1)

                each_unit(dve, EDGE_UNITS, destination_stats)
                dve.wait_ge(dst_seen, EDGE_UNITS)
                stats_to_moments(dve, dst_stats, dst_moment, moment_step, 0)
                scales(dst_moment, 0)
                for k in range(RING):
                    source_stats(0, k)
                dve.wait_ge(src_seen, RING)
                stats_to_moments(dve, src_stats, src_moment, moment_step, MOMENT_STEPS)
                scales(src_moment, 1)

                def body(i, k):
                    u, par = RING * i + k, k % 2
                    prev = ahead(i, k, -1)
                    carry = carry_steps(*prev) if exists(*prev, EDGE_UNITS) else iter(())
                    mixing = mix_steps(*prev) if exists(*prev, EDGE_UNITS) else iter(())
                    more = exists(i + 1, 0, EDGE_UNITS)
                    dve.wait_ge(q_ready, u + 1)
                    nc.vector.tensor_tensor(kq[par][:], projs[par][:, :, 0:C], q[par][:], ALU.mult).then_inc(kq_done, 1)
                    next(carry, None)
                    dve.wait_ge(in_loaded[k], 48 * (i + 1))
                    dve.wait_ge(kq_done, u + 1)
                    nc.vector.tensor_tensor(kq[par][:], e[k][:].rearrange("p (j c) -> p j c", j=J), kq[par][:], ALU.mult).then_inc(kqe_done, 1)
                    next(carry, None)
                    dve.wait_ge(kqe_done, u + 1)
                    wait(dve, weights_ready, u - 1)
                    nc.vector.reduce_sum(score[par][:], kq[par][:].rearrange("p j (h d) -> p j h d", h=HEADS), axis=AXX
                                         ).then_inc(score_summed, 1)
                    next(carry, None)
                    dve.wait_ge(score_summed, u + 1)
                    nc.vector.tensor_scalar(score[par][:], score[par][:], 5.0, -5.0, ALU.min, ALU.max).then_inc(clipped, 1)
                    if k < RING // 2:
                        for slot in (2 * k, 2 * k + 1):
                            if exists(i + 1, slot, EDGE_UNITS):
                                source_stats(i + 1, slot)
                    if k == RING // 2 - 1 and more:
                        seen = RING * (i + 2)
                        dve.wait_ge(src_seen, min(seen, EDGE_UNITS) if isinstance(i, int) else seen)
                        stats_to_moments(dve, src_stats, src_moment, moment_step, MOMENT_STEPS * (i + 2))
                    if k == RING // 2 + 1 and more:
                        dve.wait_ge(s_normed, RING * (i + 1))
                        scales(src_moment, i + 2)
                    for _ in range(3):
                        next(mixing, None)
                    dve.wait_ge(weights_ready, u + 1)
                    weights = msg[par][:, :, C:M_COLS].unsqueeze(3).to_broadcast([P, J, HEADS, HEAD_DIM])
                    nc.vector.tensor_tensor(msg[par][:, :, 0:C].rearrange("p j (h d) -> p j h d", h=HEADS),
                                            projs[par][:, :, C:2 * C].rearrange("p j (h d) -> p j h d", h=HEADS), weights,
                                            ALU.mult).then_inc(msg_ready, 1)
                    next(mixing, None)

                each_unit(dve, EDGE_UNITS, body)
                for steps in (carry_steps, mix_steps):
                    for _ in steps(*ahead(0, 0, EDGE_UNITS - 1)):
                        pass
    return nc


def kernel(x, src, dst, edge_attr_96, L0_gnn_weight, L0_gnn_w_ih, L0_gnn_w_hh, L0_gnn_b_ih, L0_gnn_b_hh,
           L1_gnn_Wq, L1_gnn_bq, L1_gnn_Wk, L1_gnn_bk, L1_gnn_We, L1_gnn_be, L1_gnn_Wv, L1_gnn_bv):
    import numpy as _np
    import concourse.bacc as _bacc
    from concourse import mybir as _mybir
    from concourse.bass_utils import run_bass_kernel_spmd as _run

    a = _np.asarray
    src, dst, edge = a(src), a(dst), a(edge_attr_96)
    w_hh, b_hh, b_ih = a(L0_gnn_w_hh), a(L0_gnn_b_hh), a(L0_gnn_b_ih)
    pad = E_PAD - N_EDGES

    def columns(v):
        return _np.ascontiguousarray(v.reshape(E_TILES, P).T)

    def n_first(v):
        return _np.concatenate([v[2 * C:], v[:2 * C]], 0)

    src_p = _np.concatenate([src, _np.zeros(pad, src.dtype)])
    dst_p = _np.concatenate([dst, _np.full(pad + 1, NO_NODE, dst.dtype)])
    arrays = {
        "x": a(x),
        "src_col": columns(src_p),
        "dst_col": columns(dst_p[:-1]),
        "dst_next_col": columns(dst_p[1:]),
        "dst_row": _np.concatenate([_np.full(1, -1, dst.dtype), dst_p[:-1]])[None, :],
        "edge_t": _np.concatenate([edge, _np.zeros((pad, C), edge.dtype)], 0).T,
        "w_t": a(L0_gnn_weight).transpose(0, 2, 1),
        "w_ih_t": a(L0_gnn_w_ih).T,
        "w_hh_t": n_first(w_hh).T,
        "b_ih": b_ih[None, :],
        "b_hh": n_first(b_hh)[None, :],
        "w_kv": _np.concatenate([a(L1_gnn_Wk), a(L1_gnn_Wv)], 1),
        "b_kv": _np.concatenate([a(L1_gnn_bk), a(L1_gnn_bv)])[None, :],
        "w_q": a(L1_gnn_Wq), "b_q": a(L1_gnn_bq)[None, :],
        "w_e": a(L1_gnn_We), "b_e": a(L1_gnn_be)[None, :],
    }
    nc = _bacc.Bacc("TRN2", target_bir_lowering=False, num_devices=1)
    feed, args = {}, []
    for name, v in arrays.items():
        v = _np.ascontiguousarray(v)
        feed[f"in_{name}"] = v
        args.append(nc.dram_tensor(f"in_{name}", v.shape, _mybir.dt.from_np(v.dtype), kind="ExternalInput").ap())
    args.append(nc.dram_tensor("out", (N_NODES + E_PAD, C), F32, kind="ExternalOutput").ap())
    build(nc, *args)
    r = _run(nc, [feed], core_ids=[0])
    return r.results[0]["out"][:N_NODES]
```
